# Optimizing a Trainium2 kernel written in Bass

```python
import numpy as np
import jax
import jax.numpy as jnp

def _softmax(x, axis=-1):
    return jax.nn.softmax(x, axis=axis)

def _gelu(x):
    return jax.nn.gelu(x, approximate=True)

def _silu(x):
    return jax.nn.silu(x)

def _sigmoid(x):
    return jax.nn.sigmoid(x)

def _layernorm(x, axis=-1, eps=1e-05):
    m = jnp.mean(x, axis=axis, keepdims=True)
    v = jnp.var(x, axis=axis, keepdims=True)
    return (x - m) / jnp.sqrt(v + eps)

def _scatter_add(tgt, idx, src, axis=0):
    return tgt.at[idx].add(src)

def _segment_sum(src, seg, n):
    return jax.ops.segment_sum(src, seg, n)
kernel_name = 'mk_xattn_ffn_d2_seqx_r4_3d3673'

def setup_inputs(seed: int=0):
    np.random.seed(seed)
    _w = jnp.asarray

    def _rec_inputs():
        import jax
        import jax.numpy as jnp
        _rk = jax.random.key(seed)
        x = 7.22e-05 + 1 * jax.random.normal(jax.random.fold_in(_rk, 1), (4, 512, 512), jnp.float32)
        _lenS = 512 - jax.random.randint(jax.random.fold_in(_rk, 7), (4,), 0, max(1, 512 // 4) + 1, jnp.int32)
        _lenS2 = 512 - jax.random.randint(jax.random.fold_in(_rk, 8), (4,), 0, max(1, 512 // 4) + 1, jnp.int32)
        _ctx_1024P = jax.random.normal(jax.random.fold_in(_rk, 11), (4, 16, 256), jnp.float32)
        _ctx_1024c = jax.random.dirichlet(jax.random.fold_in(_rk, 511), 0.3 * jnp.ones((16,), jnp.float32), (4, 512))
        _ctx_1024t = jnp.einsum('bsk,bkd->bsd', _ctx_1024c, _ctx_1024P)
        _ctx_1024t = _ctx_1024t * jax.lax.rsqrt(jnp.mean(jnp.square(_ctx_1024t)) + 1e-12) * 0.953939
        ctx_1024 = 2.81802e-05 + 1.00001 * (_ctx_1024t + 0.3 * jax.random.normal(jax.random.fold_in(_rk, 611), (4, 512, 256), jnp.float32))
        _validS = jnp.arange(512)[None, :] < _lenS[:, None]
        _validS2 = jnp.arange(512)[None, :] < _lenS2[:, None]
        _causal = jnp.tril(jnp.ones((512, 512), dtype=bool))
        mask_BxS2_bf1 = jnp.ones((4, 512), dtype=bool)
        return (x, ctx_1024, mask_BxS2_bf1)
    x, ctx_1024, mask_BxS2_bf1 = _rec_inputs()

    def _L0_xattn_setup():
        import jax, jax.numpy as jnp
        import numpy as np
        key = jax.random.key(seed)
        ks = jax.random.split(key, 6)
        B, L, N, C, D = (8, 128, 512, 256, 128)
        return {'teacher_logits': jax.random.normal(ks[0], (B, L, N), dtype=jnp.float32), 'teacher_features': jax.random.normal(ks[1], (B, N, C), dtype=jnp.float32), 'Wq': jax.random.normal(ks[2], (D, C), dtype=jnp.float32) * (1.0 / np.sqrt(C)), 'bq': jnp.zeros((D,), dtype=jnp.float32), 'Wk': jax.random.normal(ks[3], (D, C), dtype=jnp.float32) * (1.0 / np.sqrt(C)), 'bk': jnp.zeros((D,), dtype=jnp.float32)}
    _L0_xattn_all = _L0_xattn_setup()
    _L0_xattn_in = {k: v for k, v in _L0_xattn_all.items() if k in ('Wq', 'bq', 'Wk', 'bk')}
    del _L0_xattn_all

    def _L0_ffn_setup():
        import jax, jax.numpy as jnp
        import numpy as np
        B, S, D_IN, D_OUT = (4, 512, 512, 512)
        EPS = 1e-10
        key = jax.random.key(seed)
        kx, kw, kb = jax.random.split(key, 3)
        x = jax.random.normal(kx, (B, S, D_IN), dtype=jnp.float32)
        weight = jax.random.normal(kw, (D_OUT, D_IN), dtype=jnp.float32) * 0.02
        bias = jax.random.normal(kb, (D_OUT,), dtype=jnp.float32) * 0.02
        return {'x': x, 'weight': weight, 'bias': bias}
    _L0_ffn_all = _L0_ffn_setup()
    _L0_ffn_in = {k: v for k, v in _L0_ffn_all.items() if k in ('weight', 'bias')}
    del _L0_ffn_all

    def _L1_xattn_setup():
        import jax, jax.numpy as jnp
        import numpy as np
        N_HEADS = 16
        N_KV_HEADS = 8
        HEAD_DIM = 128
        D_TEXT = 512
        D_VISION = 256
        GROUPS = N_HEADS // N_KV_HEADS
        key = jax.random.key(seed)
        ks = jax.random.split(key, 6)
        B, T_text, T_vis = (4, 512, 144)
        text_hidden = jax.random.normal(ks[0], (B, T_text, D_TEXT), dtype=jnp.float32)
        vision_tokens = jax.random.normal(ks[1], (B, T_vis, D_VISION), dtype=jnp.float32)
        vision_mask = jnp.ones((B, T_vis), dtype=bool)
        s = 0.02
        Wq = jax.random.normal(ks[2], (D_TEXT, N_HEADS * HEAD_DIM), dtype=jnp.float32) * s
        Wk = jax.random.normal(ks[3], (D_VISION, N_KV_HEADS * HEAD_DIM), dtype=jnp.float32) * s
        Wv = jax.random.normal(ks[4], (D_VISION, N_KV_HEADS * HEAD_DIM), dtype=jnp.float32) * s
        Wo = jax.random.normal(ks[5], (N_HEADS * HEAD_DIM, D_TEXT), dtype=jnp.float32) * s
        return {'text_hidden': text_hidden, 'vision_tokens': vision_tokens, 'vision_mask': vision_mask, 'Wq': Wq, 'Wk': Wk, 'Wv': Wv, 'Wo': Wo}
    _L1_xattn_all = _L1_xattn_setup()
    _L1_xattn_in = {k: v for k, v in _L1_xattn_all.items() if k in ('Wq', 'Wk', 'Wv', 'Wo')}
    del _L1_xattn_all

    def _L1_ffn_setup():
        import jax, jax.numpy as jnp
        import numpy as np

        def _sparsify_2to4(h):
            B, S, I = h.shape
            g = h.reshape(B, S, I // 4, 4)
            a = jnp.abs(g)
            _, idx = jax.lax.top_k(a, 2)
            pos = jnp.arange(4)
            mask = (pos == idx[..., 0:1]) | (pos == idx[..., 1:2])
            return (g * mask.astype(g.dtype)).reshape(B, S, I)
        key = jax.random.key(seed)
        k1, k2, k3, k4 = jax.random.split(key, 4)
        B, S, H, I = (4, 512, 512, 2048)
        x = jax.random.normal(k1, (B, S, H), dtype=jnp.float32)
        w_gate = jax.random.normal(k2, (H, I), dtype=jnp.float32) / np.sqrt(H)
        w_up = jax.random.normal(k3, (H, I), dtype=jnp.float32) / np.sqrt(H)
        w_down = jax.random.normal(k4, (I, H), dtype=jnp.float32) / np.sqrt(I)
        return {'x': x, 'w_gate': w_gate, 'w_up': w_up, 'w_down': w_down}
    _L1_ffn_all = _L1_ffn_setup()
    _L1_ffn_in = {k: v for k, v in _L1_ffn_all.items() if k in ('w_gate', 'w_up', 'w_down')}
    del _L1_ffn_all
    return {'x': x, 'ctx_1024': ctx_1024, 'mask_BxS2_bf1': mask_BxS2_bf1, 'L0_xattn_Wq': _L0_xattn_in['Wq'], 'L0_xattn_bq': _L0_xattn_in['bq'], 'L0_xattn_Wk': _L0_xattn_in['Wk'], 'L0_xattn_bk': _L0_xattn_in['bk'], 'L0_ffn_weight': _L0_ffn_in['weight'], 'L0_ffn_bias': _L0_ffn_in['bias'], 'L1_xattn_Wq': _L1_xattn_in['Wq'], 'L1_xattn_Wk': _L1_xattn_in['Wk'], 'L1_xattn_Wv': _L1_xattn_in['Wv'], 'L1_xattn_Wo': _L1_xattn_in['Wo'], 'L1_ffn_w_gate': _L1_ffn_in['w_gate'], 'L1_ffn_w_up': _L1_ffn_in['w_up'], 'L1_ffn_w_down': _L1_ffn_in['w_down']}

def reference(x, ctx_1024, mask_BxS2_bf1, L0_xattn_Wq, L0_xattn_bq, L0_xattn_Wk, L0_xattn_bk, L0_ffn_weight, L0_ffn_bias, L1_xattn_Wq, L1_xattn_Wk, L1_xattn_Wv, L1_xattn_Wo, L1_ffn_w_gate, L1_ffn_w_up, L1_ffn_w_down):
    import jax
    import jax.numpy as jnp

    def _L0_xattn_ref(teacher_logits, teacher_features, Wq, bq, Wk, bk):
        import jax, jax.numpy as jnp
        import numpy as np
        query = jnp.einsum('bnc,dc->bnd', teacher_features, Wq) + bq
        key = jnp.einsum('bnc,dc->bnd', teacher_features, Wk) + bk
        energy = jnp.einsum('bnd,bmd->bnm', query, key)
        attention = jax.nn.softmax(energy, axis=-1)
        x_m = jnp.einsum('bln,bmn->blm', teacher_logits, attention)
        return x_m

    def _L0_ffn_ref(x, weight, bias):
        import jax, jax.numpy as jnp
        import numpy as np
        B, S, D_IN, D_OUT = (4, 512, 512, 512)
        EPS = 1e-10
        scale = jnp.mean(jnp.abs(weight))
        w_t = jnp.clip(jnp.round(weight / (scale + EPS)), -1.0, 1.0)
        w_ste = weight + jax.lax.stop_gradient(w_t * scale - weight)
        return jnp.einsum('bsi,oi->bso', x, w_ste) + bias

    def _L1_xattn_ref(text_hidden, vision_tokens, vision_mask, Wq, Wk, Wv, Wo):
        import jax, jax.numpy as jnp
        import numpy as np
        N_HEADS = 16
        N_KV_HEADS = 8
        HEAD_DIM = 128
        D_TEXT = 512
        D_VISION = 256
        GROUPS = N_HEADS // N_KV_HEADS
        B, T_text, _ = text_hidden.shape
        T_vis = vision_tokens.shape[1]
        scale = jnp.float32(np.sqrt(HEAD_DIM))
        q = (text_hidden @ Wq).reshape(B, T_text, N_HEADS, HEAD_DIM).transpose(0, 2, 1, 3)
        k = (vision_tokens @ Wk).reshape(B, T_vis, N_KV_HEADS, HEAD_DIM).transpose(0, 2, 1, 3)
        v = (vision_tokens @ Wv).reshape(B, T_vis, N_KV_HEADS, HEAD_DIM).transpose(0, 2, 1, 3)
        k = jnp.repeat(k, GROUPS, axis=1)
        v = jnp.repeat(v, GROUPS, axis=1)
        scores = jnp.einsum('bhtd,bhsd->bhts', q, k) / scale
        mask = vision_mask[:, None, None, :]
        scores = jnp.where(mask, scores, -jnp.inf)
        attn = jax.nn.softmax(scores, axis=-1)
        attn = jnp.nan_to_num(attn, nan=0.0)
        out = jnp.einsum('bhts,bhsd->bhtd', attn, v)
        out = out.transpose(0, 2, 1, 3).reshape(B, T_text, N_HEADS * HEAD_DIM)
        return out @ Wo

    def _L1_ffn_ref(x, w_gate, w_up, w_down):
        import jax, jax.numpy as jnp
        import numpy as np

        def _sparsify_2to4(h):
            B, S, I = h.shape
            g = h.reshape(B, S, I // 4, 4)
            a = jnp.abs(g)
            _, idx = jax.lax.top_k(a, 2)
            pos = jnp.arange(4)
            mask = (pos == idx[..., 0:1]) | (pos == idx[..., 1:2])
            return (g * mask.astype(g.dtype)).reshape(B, S, I)
        h = jax.nn.silu(jnp.einsum('bsh,hi->bsi', x, w_gate)) * jnp.einsum('bsh,hi->bsi', x, w_up)
        h_sparse = _sparsify_2to4(h)
        return jnp.einsum('bsi,ih->bsh', h_sparse, w_down)
    x = x + _L0_xattn_ref(_layernorm(x, axis=-1), ctx_1024, L0_xattn_Wq, L0_xattn_bq, L0_xattn_Wk, L0_xattn_bk)
    x = x + _L0_ffn_ref(_layernorm(x, axis=-1), L0_ffn_weight, L0_ffn_bias)
    x = x + _L1_xattn_ref(_layernorm(x, axis=-1), ctx_1024, mask_BxS2_bf1, L1_xattn_Wq, L1_xattn_Wk, L1_xattn_Wv, L1_xattn_Wo)
    x = x + _L1_ffn_ref(_layernorm(x, axis=-1), L1_ffn_w_gate, L1_ffn_w_up, L1_ffn_w_down)
    return x

_drawn_inputs = setup_inputs


def setup_inputs(seed=0):
    import zlib

    import numpy as np

    out = dict(_drawn_inputs(seed))
    spreads = {'L0_xattn_bq': (0.0, 0.1), 'L0_xattn_bk': (0.0, 0.8)}
    factors = {'L1_xattn_Wq': 5.242, 'L1_xattn_Wk': 5.288}
    for name, (base, spread) in spreads.items():
        noise = np.random.default_rng([zlib.crc32(name.encode()), seed]).standard_normal(out[name].shape)
        drawn = base * np.exp(spread * noise) if base else spread * noise
        out[name] = jnp.asarray(drawn.astype(out[name].dtype))
    for name, factor in factors.items():
        out[name] = (out[name] * factor).astype(out[name].dtype)
    return out
```

```python
from contextlib import ExitStack

import concourse.bass as bass
from concourse import mybir

F32 = mybir.dt.float32
F32R = mybir.dt.float32r
BF16 = mybir.dt.bfloat16
U8 = mybir.dt.uint8
ALU = mybir.AluOpType
ACT = mybir.ActivationFunctionType
AX_X = mybir.AxisListType.X

P = 128
B, S, D, C = 4, 512, 512, 256
NT = S // P
KD, KC = D // P, C // P
GROUPS, HPG, DH = 8, 2, 128
HIDDEN, CHUNK = 2048, 512
CHUNKS, NR = HIDDEN // CHUNK, 4
PAIRS = B // 2
LN_EPS = 1e-5
TERNARY_EPS = 1e-10
SCORE_SCALE = float(DH) ** -0.5
MASKED = 3e38
MIN_START = 3.4e38

def first_layers_order():
    both = (0, 1)
    o = [("NO_MASK",)] + [("LN", b) for b in both] + [("SPLIT_W0",)]
    o += [("CT", b, c) for b in both for c in range(KC)]
    for b in both:
        o += [("K0", b), ("Q0", b)]
    for b in both:
        o += [("E", b, i) for i in range(NT)] + [("RS", b, b)]
        o += [("XT", b, j) for j in range(KD)]
    for b in both:
        o += [("AT", b, j) for j in range(NT)] + [("XM", b, i) for i in range(NT)] + [("LN", b)]
    o += [("ADD_BIAS",)]
    for b in both:
        o += [("XT", b, j) for j in range(KD)] + [("FC", b, i) for i in range(NT)] + [("LN", b)]
    for b in both:
        o += [("XT", b, j) for j in range(KD)]
    return o


def weave(b, h, fill):
    t, v = [("T", b, h, j) for j in range(NT)], [("PV", b, h, j) for j in range(NT)]
    q = [fill[i * len(fill) // 5:(i + 1) * len(fill) // 5] for i in range(5)]
    return [t[0], t[1], *q[0], v[0], t[2], *q[1], v[1], t[3], *q[2], v[2], *q[3], v[3], *q[4]]


def scores(b, h):
    return [("S", b, h, i) for i in range(NT)]


def group_prologue():
    return [("MASK",), ("WQKV",), ("K", 0), ("Q", 0, 0), *scores(0, 0), ("RS", 0, 0), ("VT", 0), ("TV", 0), ("Q", 0, 1)]


def group_order(first, last):
    prev = [] if first else [("Y", 1, i) for i in range(NT)]
    y0 = [("Y", 0, i) for i in range(NT)]
    s01, s10, s11 = scores(0, 1), scores(1, 0), scores(1, 1)
    o = weave(0, 0, [*s01[:3], ("K", 1), s01[3], ("Q", 1, 0), ("RS", 1, 0), *prev[:2]])
    o += weave(0, 1, [*s10[:2], ("VT", 1), s10[2], s10[3], ("TV", 1), ("Q", 1, 1), ("RS", 0, 1), *prev[2:]])
    o += [("WO",)]
    if last:
        o += weave(1, 0, [*s11, ("RS", 1, 1), *y0])
        o += weave(1, 1, [])
        o += [("Y", 1, i) for i in range(NT)]
        return o
    o += [("WQKV",)]
    n00 = scores(0, 0)
    o += weave(1, 0, [*s11[:3], y0[0], s11[3], y0[1], ("K", 0), ("RS", 1, 1), ("Q", 0, 0)])
    o += weave(1, 1, [*n00[:2], ("VT", 0), n00[2], n00[3], ("TV", 0), ("Q", 0, 1), ("RS", 0, 0), *y0[2:]])
    return o


def mlp_prologue():
    o = [("LN", b) for b in (0, 1)] + [("WP", p) for p in range(6)]
    return o + [("XT", b, j) for b in (0, 1) for j in range(KD)]


def mlp_order(last):
    o = []
    for b in (0, 1):
        o += [("GU", b, r) for r in range(NR)] + [("KEEP", b)]
    if not last:
        o += [("WP", p) for p in range(4)]
    for b in (0, 1):
        o += [("DN", b, i) for i in range(NT)]
    if not last:
        o += [("WP", p) for p in (4, 5)]
    return o


MOVES = {
    "NO_MASK": {"step": 1}, "MASK": {"step": 2}, "ADD_BIAS": {"step": 1},
    "LN": {"step": NT, "stat": 1, "rstd": 2, "xn": NT},
    "SPLIT_W0": {"hi": 1, "w": 1}, "WQKV": {"hi": 3, "w": 3, "qkv": 48}, "WO": {"hi": 1, "w": 1, "wol": 16},
    "CT": {"t": 1, "hi": 1}, "XT": {"t": 1, "hi": 1}, "AT": {"t": 1, "hi": 1}, "T": {"t": 1, "hi": 1},
    "TV": {"t": 1, "hi": 1}, "K0": {"pj": 1, "hi": 1}, "Q0": {"pj": 1, "hi": 1}, "K": {"pj": 1, "hi": 1},
    "Q": {"pj": 1, "hi": 1}, "VT": {"pj": 1}, "E": {"s": 1, "exp": 1}, "S": {"s": 1, "exp": 1},
    "RS": {"rs": 1, "norm": NT}, "XM": {"y": 1}, "FC": {"y": 1}, "Y": {"y": 1},
    "GU": {"gu": 1, "sg": 1, "ab": 1}, "KEEP": {"kept": NR, "hi": NR, "hs": NR, "step": 11}, "DN": {"yf": 1},
}


def moves(e):
    if e[0] == "PV":
        return {"o": 1, "hi": 1} if e[3] == NT - 1 else {}
    if e[0] == "WP":
        return {"fw": 1, "hi": 1, f"piece{e[1] % 3}": 16}
    return MOVES[e[0]]


def total_moves(order):
    out = {}
    for e in order:
        for k, v in moves(e).items():
            out[k] = out.get(k, 0) + v
    return out


class Counts:

    def __init__(self, eng, used):
        self.eng, self.used = eng, used
        self.n, self.past, self.base = {}, {}, {k: 0 for k in used}

    def step(self, e):
        at = {k: self.n.get(k, 0) for k in moves(e)}
        for k, v in moves(e).items():
            self.n[k] = at[k] + v
        return at

    def value(self, k, n):
        return self.base[k] + n

    def loop(self, reg, per):
        outer = dict(self.base)
        for k in self.used:
            if per.get(k):
                self.base[k] = self.eng.snap(reg * per[k] + self.base[k])
        return outer

    def after_loop(self, outer, per, trips):
        self.base = outer
        for k, v in per.items():
            self.past[k] = self.past.get(k, 0) + v * (trips - 1)
            if k in self.used:
                self.base[k] = self.eng.snap(outer[k] + v * (trips - 1))


PER_GROUP = total_moves(group_order(False, False))
PER_CHUNK = total_moves(mlp_order(False))
PER_PAIR = total_moves(first_layers_order() + group_prologue() + group_order(True, False)
                       + group_order(False, False) * (GROUPS - 2) + group_order(False, True)
                       + mlp_prologue() + mlp_order(False) * (CHUNKS - 1) + mlp_order(True))


def build(nc, x_in, ctx_in, mask_in, wq0_in, bq0_in, wk0_in, bk0_in, w0_in, b0_in,
          wq_in, wk_in, wv_in, wo_in, wg_in, wu_in, wd_in, out):
    x_rows = x_in.rearrange("(q b) (i p) d -> q p b i d", b=2, p=P)
    out_rows = out.rearrange("(q b) (i p) d -> q p b i d", b=2, p=P)
    ctx_rows = ctx_in.rearrange("(q b) (i p) c -> q p b i c", b=2, p=P)
    mask_rows = mask_in.rearrange("(q b) s -> q b s", b=2)
    wq_cols = wq_in.rearrange("(k p) n -> p k n", p=P)
    wk_cols = wk_in.rearrange("(k p) n -> p k n", p=P)
    wv_cols = wv_in.rearrange("(k p) n -> p k n", p=P)
    wo_rows = wo_in.rearrange("(g h d) n -> g d h n", g=GROUPS, h=HPG)
    wg_cols = wg_in.rearrange("(k p) n -> p k n", p=P)
    wu_cols = wu_in.rearrange("(k p) n -> p k n", p=P)
    wd_rows = wd_in.rearrange("(c j r) n -> c j r n", c=CHUNKS, r=NR)

    with ExitStack() as es:
        def sb(name, shape, dt=F32):
            return es.enter_context(nc.sbuf_tensor(name, shape, dt))

        x = sb("x", [P, 2, NT, D])
        ident = sb("ident", [P, P])
        w0_t = sb("w0_t", [P, KD, D])
        bias0 = sb("bias0", [P, D])
        mask_add = sb("mask_add", [P, 2, S])
        mask_u8 = sb("mask_u8", [P, 2, S], U8)
        any_valid = sb("any_valid", [P, 2])
        small = sb("small", [P, 8])
        nbq, bk = small[:, 0:1], small[:, 1:2]
        total, scale0, cut, ncut = small[:, 2:3], small[:, 3:4], small[:, 4:5], small[:, 5:6]
        marks = sb("marks", [P, 16])
        ones = sb("ones", [P, P])
        half = sb("half", [P, NT])
        smin, ssum, srec = sb("smin", [P, 2, NT]), sb("ssum", [P, 2, NT]), sb("srec", [P, 2, NT])
        bn = sb("bn", [P, NT, 6])
        mv = sb("mv", [P, 2, NT, 2])
        rstd = sb("rstd", [P, 2, NT])
        xn = sb("xn", [P, 2, NT, D])
        prob = sb("prob", [P, 2, NT, S])
        raw = sb("raw", [P, 3, 2 * D])
        xt = sb("xt", [P, 2, 2, KD, S], F32R)
        wqk0 = sb("wqk0", [P, 2, 2, KC, P], F32R)
        area = sb("area", [P, 92 * 256], F32R)

        def half_views(at, *shape):
            n = 1
            for m in shape:
                n *= m
            names = "abcd"[:len(shape)]
            out = []
            for k in range(2):
                v = area[:, at + k * n:at + (k + 1) * n]
                if len(shape) > 1:
                    v = v.rearrange(f"p ({' '.join(names)}) -> p {' '.join(names)}", **dict(zip(names, shape)))
                out.append(v)
            return out, at + 2 * n

        ctx_t, at = half_views(0, 2, KC, S)
        q_t, at = half_views(at, 2, HPG, S)
        k_t, at = half_views(at, 2, S)
        w0_at = at
        v_s, at = half_views(at, 2, NT, DH)
        p_t, at = half_views(at, 2, S)
        o_t, at = half_views(at, 2, HPG, S)
        wq, at = half_views(at, KD, HPG * DH)
        wk, at = half_views(at, KC, DH)
        wv, at = half_views(at, KC, DH)
        wo, at = half_views(at, HPG, D)
        assert at <= 92 * 256
        w0, _ = half_views(w0_at, KD, D)
        att_t, _ = half_views(w0_at + 4096, NT, S)
        wg, at = half_views(0, KD, CHUNK)
        wu, at = half_views(at, KD, CHUNK)
        wd, at = half_views(at, NR, D)
        h_t, at = half_views(at, 2, NR, S)
        assert at <= 92 * 256
        ctx_raw = prob[:, 0, :, :].rearrange("p i d -> p (i d)").rearrange("p (b i c) -> p b i c", b=2, i=NT)
        raw_flat = raw[:, :, :].rearrange("p a n -> p (a n)")
        nq, nk = KD * HPG * DH, KC * DH
        raw_q = raw_flat[:, 0:nq].rearrange("p (k n) -> p k n", k=KD)
        raw_k = raw_flat[:, nq:nq + nk].rearrange("p (k n) -> p k n", k=KC)
        raw_v = raw_flat[:, nq + nk:nq + 2 * nk].rearrange("p (k n) -> p k n", k=KC)
        raw_o = raw_flat[:, nq + 2 * nk:nq + 2 * nk + HPG * D].rearrange("p (h n) -> p h n", h=HPG)
        v_tmp = raw_flat[:, nq + 2 * nk + HPG * D:nq + 2 * nk + HPG * D + S]
        w0_raw = xn[:, 0]
        w0_ste = xn[:, 1]
        wqk0_raw = prob[:, 1, 0:2, 0:C]
        h_f, h_abs = prob[:, 0], prob[:, 1]
        silu = xn[:, 0, 0:2]
        flags = xn[:, :, :, :].rearrange("p a i d -> p (a i d)")[:, 1024:].bitcast(BF16)\
            .rearrange("p (c n) -> p c n", n=S)

        bank = [es.enter_context(nc.psum_tensor(f"bank{i}", [P, 512], F32)) for i in range(8)]
        proj_ps, score_ps, tr_ps, o_ps, y_ps = bank[0:2], bank[2:4], bank[4:6], bank[6], bank[7]
        gate_ps, up_ps, down_ps = bank[2:4], bank[0:2], bank[6:8]

        def sem(name):
            return es.enter_context(nc.semaphore(name))

        full = {k: sem(f"{k}_full") for k in ("pj", "s", "t", "o", "y", "gu", "yf")}
        taken = {k: sem(f"{k}_taken") for k in ("pj", "s", "t", "o", "y", "gu", "yf")}
        SLOTS = {"pj": 2, "s": 2, "t": 2, "o": 1, "y": 1, "gu": 2, "yf": 2}
        hi_done, exp_done, rs_done, norm_done = sem("hi_done"), sem("exp_done"), sem("rs_done"), sem("norm_done")
        stats_done, rstd_done, xn_done = sem("stats_done"), sem("rstd_done"), sem("xn_done")
        silu_done, abs_done, kept_done, h_split = sem("silu_done"), sem("abs_done"), sem("kept_done"), sem("h_split")
        w_split, mlp_w_split = sem("w_split"), sem("mlp_w_split")
        x_landed, ctx_landed, mask_landed = sem("x_landed"), sem("ctx_landed"), sem("mask_landed")
        qkv_landed, wo_landed = sem("qkv_landed"), sem("wo_landed")
        mlp_landed = [sem(f"mlp_landed{i}") for i in range(3)]
        stored, setup_landed, phase_done = sem("stored"), sem("setup_landed"), sem("phase_done")
        ident_done, ternary_done, ternary_step, setup_sum, setup_t, setup_taken, setup_hi, dve_step = (
            sem("ident_done"), sem("ternary_done"), sem("ternary_step"), sem("setup_sum"), sem("setup_t"), sem("setup_taken"),
            sem("setup_hi"), sem("dve_step"))

        def run(eng, cnt, steps):
            with eng.Fori(0, PAIRS) as pair:
                outer = cnt.loop(pair, PER_PAIR)
                done = eng.snap(pair * 3)
                eng.wait_ge(phase_done, done + 1)
                steps("first", first_layers_order(), pair)
                eng.wait_ge(phase_done, done + 2)
                steps("attention", group_prologue() + group_order(True, False), pair)
                with eng.Fori(1, GROUPS - 1) as g:
                    before = cnt.loop(eng.snap(g - 1), PER_GROUP)
                    steps("attention", group_order(False, False), pair)
                cnt.after_loop(before, PER_GROUP, GROUPS - 2)
                steps("attention end", group_order(False, True), pair)
                eng.wait_ge(phase_done, done + 3)
                steps("mlp", mlp_prologue(), pair)
                with eng.Fori(0, CHUNKS - 1) as c:
                    before = cnt.loop(c, PER_CHUNK)
                    steps("mlp", mlp_order(False), pair)
                cnt.after_loop(before, PER_CHUNK, CHUNKS - 1)
                steps("mlp end", mlp_order(True), pair)
                assert all(cnt.n[k] + cnt.past.get(k, 0) == v for k, v in PER_PAIR.items())
            cnt.base = outer

        def stand(eng):
            eng.nop(nofuse=True)

        def part(halves, *ix):
            return [v[(slice(None), *ix)] for v in halves]

        block = es.enter_context(nc.Block())

        @block.sync
        def _(sp):
            sp.dma_start(w0_raw, w0_in.rearrange("(a p) n -> p a n", p=P)).then_inc(setup_landed, 16)
            sp.dma_start(wqk0_raw[:, 0], wq0_in).then_inc(setup_landed, 16)
            sp.dma_start(wqk0_raw[:, 1], wk0_in).then_inc(setup_landed, 16)
            sp.dma_start(bias0[:, :], b0_in.rearrange("(a n) -> a n", a=1).to_broadcast([P, D])).then_inc(setup_landed, 16)
            sp.dma_start(small[:, 6:7], bq0_in.rearrange("(p a) -> p a", a=1)).then_inc(setup_landed, 16)
            sp.dma_start(bk, bk0_in.rearrange("(p a) -> p a", a=1)).then_inc(setup_landed, 16)

            with sp.Fori(0, PAIRS) as pair:
                done = sp.snap(pair * 3)
                w_base = sp.snap(pair * PER_PAIR["w"])
                fw_base = sp.snap(pair * PER_PAIR["fw"])
                sp.wait_ge(phase_done, done + 1)
                stand(sp)
                sp.dma_start(x[:, :, :, :], x_rows[bass.ds(pair, 1)][0]).then_inc(x_landed, 16)
                sp.dma_start(ctx_raw, ctx_rows[bass.ds(pair, 1)][0]).then_inc(ctx_landed, 16)
                for b in range(2):
                    sp.dma_start(mask_u8[:, b, :], mask_rows[bass.ds(pair, 1), b, :].to_broadcast([P, S]))\
                        .then_inc(mask_landed, 16)

                def load_qkv(g):
                    sp.dma_start(raw_q, wq_cols[:, :, bass.ds(g * (HPG * DH), HPG * DH)]).then_inc(qkv_landed, 16)
                    sp.dma_start(raw_k, wk_cols[:, :, bass.ds(g * DH, DH)]).then_inc(qkv_landed, 16)
                    sp.dma_start(raw_v, wv_cols[:, :, bass.ds(g * DH, DH)]).then_inc(qkv_landed, 16)

                def load_wo(g):
                    sp.dma_start(raw_o, wo_rows[bass.ds(g, 1)][0]).then_inc(wo_landed, 16)

                load_qkv(0)
                load_wo(0)
                with sp.Fori(1, GROUPS) as g:
                    split = sp.snap(g * 4 + w_base)
                    sp.wait_ge(w_split, split)
                    stand(sp)
                    load_qkv(g)
                    sp.wait_ge(w_split, split + 1)
                    stand(sp)
                    load_wo(g)
                sp.wait_ge(phase_done, done + 3)
                stand(sp)

                def load_piece(piece, c, landed):
                    dst = raw[:, piece % 3, :].rearrange("p (k n) -> p k n", k=2)
                    if piece < 4:
                        src = (wg_cols, wu_cols)[piece % 2][:, 2 * (piece // 2):2 * (piece // 2) + 2,
                                                            bass.ds(c * CHUNK, CHUNK)]
                    else:
                        src = wd_rows[bass.ds(c, 1)][0][:, 2 * (piece - 4):2 * (piece - 4) + 2, :]
                    sp.dma_start(dst, src).then_inc(mlp_landed[piece % 3], 16)

                for piece in range(3):
                    load_piece(piece, 0, None)
                for piece in range(3, 6):
                    sp.wait_ge(mlp_w_split, fw_base + (piece - 2))
                    stand(sp)
                    load_piece(piece, 0, None)
                with sp.Fori(1, CHUNKS) as c:
                    split = sp.snap(c * 6 + fw_base)
                    for piece in range(6):
                        sp.wait_ge(mlp_w_split, split + (piece - 2))
                        stand(sp)
                        load_piece(piece, c, None)
                sp.wait_ge(phase_done, done + 4)
                stand(sp)
                sp.dma_start(out_rows[bass.ds(pair, 1)][0], x[:, :, :, :]).then_inc(stored, 16)
                stores = sp.snap(pair * 16)
                sp.wait_ge(stored, stores + 16)
                stand(sp)

        @block.gpsimd
        def _(pool):
            pool.memset(ident[:, :], 0.0).then_inc(ident_done, 1)
            pool.memset(ones[:, :], 1.0).then_inc(ident_done, 1)
            pool.memset(half[:, :], -0.5).then_inc(ident_done, 1)
            pool.wait_ge(ident_done, 3)
            pool.affine_select(out=ident[:, :], in_=ident[:, :], compare_op=ALU.not_equal, fill=1.0, base=0,
                               pattern=[[-1, P]], channel_multiplier=1).then_inc(ident_done, 1)
            cnt = Counts(pool, ("stat", "rstd", "rs"))

            def steps(kind, order, pair):
                for e in order:
                    at = cnt.step(e)
                    if e[0] == "LN":
                        b = e[1]
                        pool.wait_ge(stats_done, cnt.value("stat", at["stat"] + 1))
                        stand(pool)
                        pool.tensor_scalar(rstd[:, b], mv[:, b, :, 1], LN_EPS, None, ALU.add).then_inc(rstd_done, 1)
                        pool.wait_ge(rstd_done, cnt.value("rstd", at["rstd"] + 1))
                        pool.tensor_tensor(rstd[:, b], rstd[:, b], half[:, :], ALU.pow).then_inc(rstd_done, 1)
                    elif e[0] == "RS":
                        u, b = e[1:]
                        pool.wait_ge(rs_done, cnt.value("rs", at["rs"] + 1))
                        stand(pool)
                        for i in range(NT):
                            if kind == "first":
                                pool.tensor_scalar(prob[:, u, i, :], prob[:, u, i, :], srec[:, u, i:i + 1], None,
                                                   ALU.mult).then_inc(norm_done, 1)
                            else:
                                pool.tensor_scalar(prob[:, u, i, :], prob[:, u, i, :], srec[:, u, i:i + 1],
                                                   any_valid[:, b:b + 1], ALU.mult, ALU.mult).then_inc(norm_done, 1)

            run(pool, cnt, steps)

        def three(a, b):
            return ((a[0], b[0]), (a[0], b[1]), (a[1], b[0]))

        @block.tensor
        def _(pe):
            cnt = Counts(pe, ("pj", "s", "t", "o", "y", "gu", "yf", "norm", "xn", "w", "fw", "hs"))
            made = {}

            def claim(ring, n):
                pe.wait_ge(taken[ring], cnt.value(ring, n + 1))

            def ready(ring, n):
                pe.wait_ge(taken[ring], cnt.value(ring, n + 1 + SLOTS[ring]))

            def products(dst, pairs):
                ops = [h for a, b in pairs for h in three(a, b)]
                for i, (w, m) in enumerate(ops):
                    last = nc.tensor.matmul(dst, w, m, start=i == 0, stop=i == len(ops) - 1)
                return last

            xt_b = [[xt[:, k, b] for k in range(2)] for b in range(2)]
            wq0t = [wqk0[:, k, 0] for k in range(2)]
            wk0t = [wqk0[:, k, 1] for k in range(2)]

            pe.wait_ge(ident_done, 4)
            pe.wait_ge(ternary_done, 1)
            nc.tensor.matmul(y_ps[:, 0:1], ones[:, :], total, start=True, stop=True).then_inc(setup_sum, 1)
            pe.wait_ge(ternary_done, 2)
            for j in range(KD):
                if j >= 2:
                    pe.wait_ge(setup_taken, j - 1)
                for i in range(KD):
                    last = nc.tensor.transpose(tr_ps[j % 2][:, i * P:(i + 1) * P], w0_ste[:, i, j * P:(j + 1) * P],
                                               ident[:, :])
                last.then_inc(setup_t, 1)
            for m in range(2):
                for c in range(KC):
                    last = nc.tensor.transpose(score_ps[m][:, c * P:(c + 1) * P], wqk0_raw[:, m, c * P:(c + 1) * P],
                                               ident[:, :])
                last.then_inc(setup_t, 1)

            def transpose4(n, src):
                for i in range(NT):
                    last = nc.tensor.transpose(tr_ps[n % 2][:, i * P:(i + 1) * P], src(i), ident[:, :])
                last.then_inc(full["t"], 1)

            def steps(kind, order, pair):
                for e in order:
                    op, at = e[0], cnt.step(e)
                    if op == "CT":
                        b, c = e[1:]
                        if (b, c) == (0, 0):
                            pe.wait_ge(ctx_landed, pe.snap(pair * 16) + 16)
                        claim("t", at["t"])
                        transpose4(at["t"], lambda i: ctx_raw[:, b, i, c * P:(c + 1) * P])
                        made["ct", b] = at["t"]
                    elif op in ("K0", "Q0"):
                        b = e[1]
                        ready("t", made["ct", b])
                        claim("pj", at["pj"])
                        w = wk0t if op == "K0" else wq0t
                        products(proj_ps[at["pj"] % 2][:, :], [(part(w, c), part(ctx_t, b, c)) for c in range(KC)])\
                            .then_inc(full["pj"], 1)
                        made["q", b, 0] = at["pj"]
                    elif op in ("E", "S"):
                        b, h, i = e[1:] if op == "S" else (e[1], 0, e[2])
                        if i == 0:
                            ready("pj", made["q", b, h])
                        claim("s", at["s"])
                        products(score_ps[at["s"] % 2][:, :], [(part(q_t, b, h, slice(i * P, (i + 1) * P)), part(k_t, b))])\
                            .then_inc(full["s"], 1)
                    elif op == "LN":
                        made["xn", e[1]] = at["xn"] + NT
                    elif op == "XT":
                        b, j = e[1:]
                        if j == 0:
                            pe.wait_ge(xn_done, cnt.value("xn", made["xn", b]))
                        claim("t", at["t"])
                        transpose4(at["t"], lambda i: xn[:, b, i, j * P:(j + 1) * P])
                        made["xt", b] = at["t"]
                    elif op == "RS":
                        made["norm", e[1]] = at["norm"] + NT
                    elif op in ("AT", "T"):
                        u, j = (e[1], e[2]) if op == "AT" else (e[2], e[3])
                        if j == 0:
                            pe.wait_ge(norm_done, cnt.value("norm", made["norm", u]))
                        claim("t", at["t"])
                        transpose4(at["t"], lambda i: prob[:, u, i, j * P:(j + 1) * P])
                        made["t", j] = at["t"]
                    elif op == "XM":
                        b, i = e[1:]
                        if i == 0:
                            ready("t", made["t", NT - 1])
                        claim("y", at["y"])
                        products(y_ps[:, :], [(part(xt_b[b], j, slice(i * P, (i + 1) * P)), part(att_t, j))
                                              for j in range(NT)]).then_inc(full["y"], 1)
                    elif op == "FC":
                        b, i = e[1:]
                        if i == 0:
                            ready("t", made["xt", b])
                        claim("y", at["y"])
                        products(y_ps[:, :], [(part(xt_b[b], j, slice(i * P, (i + 1) * P)), part(w0, j))
                                              for j in range(KD)]).then_inc(full["y"], 1)
                    elif op == "WQKV":
                        made["wqkv"] = at["w"] + 3
                    elif op == "WO":
                        made["wo"] = at["w"] + 1
                    elif op in ("K", "VT", "Q"):
                        b = e[1]
                        if op == "K" and b == 0:
                            pe.wait_ge(w_split, cnt.value("w", made["wqkv"]))
                        claim("pj", at["pj"])
                        made[e] = at["pj"]
                        if op == "Q":
                            h = e[2]
                            args = [(part(wq, k, slice(h * DH, (h + 1) * DH)), part(xt_b[b], k)) for k in range(KD)]
                            made["q", b, h] = at["pj"]
                        else:
                            args = [(part(wk if op == "K" else wv, c), part(ctx_t, b, c)) for c in range(KC)]
                        products(proj_ps[at["pj"] % 2][:, :], args).then_inc(full["pj"], 1)
                    elif op == "TV":
                        ready("pj", made["VT", e[1]])
                        claim("t", at["t"])
                        transpose4(at["t"], lambda i: v_tmp[:, i * P:(i + 1) * P])
                    elif op == "PV":
                        b, h, j = e[1:]
                        if j == 0:
                            claim("o", cnt.n.get("o", 0))
                        ready("t", made["t", j])
                        ops = three(part(v_s, b, j), part(p_t, j % 2))
                        for k, (w, m) in enumerate(ops):
                            last = nc.tensor.matmul(o_ps[:, :], w, m, start=(j, k) == (0, 0), stop=(j, k) == (NT - 1, 2))
                        if j == NT - 1:
                            last.then_inc(full["o"], 1)
                            made["o", b] = at["o"]
                    elif op == "Y":
                        b, i = e[1:]
                        if i == 0:
                            ready("o", made["o", b])
                            pe.wait_ge(w_split, cnt.value("w", made["wo"]))
                        claim("y", at["y"])
                        products(y_ps[:, :], [(part(o_t, b, h, slice(i * P, (i + 1) * P)), part(wo, h))
                                              for h in range(HPG)]).then_inc(full["y"], 1)
                    elif op == "WP":
                        made["piece", e[1]] = at["fw"] + 1
                    elif op == "GU":
                        b, r = e[1:]
                        if (b, r) == (0, 0):
                            pe.wait_ge(mlp_w_split, cnt.value("fw", made["piece", 3]))
                            ready("t", made["xt", 1])
                        claim("gu", at["gu"])
                        cols = slice(r * P, (r + 1) * P)
                        products(gate_ps[at["gu"] % 2][:, :], [(part(wg, k, cols), part(xt_b[b], k)) for k in range(KD)])
                        products(up_ps[at["gu"] % 2][:, :], [(part(wu, k, cols), part(xt_b[b], k)) for k in range(KD)])\
                            .then_inc(full["gu"], 1)
                    elif op == "KEEP":
                        made["h", e[1]] = at["hs"] + NR
                    elif op == "DN":
                        b, i = e[1:]
                        if (b, i) == (0, 0):
                            pe.wait_ge(mlp_w_split, cnt.value("fw", made["piece", 5]))
                        if i == 0:
                            pe.wait_ge(h_split, cnt.value("hs", made["h", b] + 1))
                        claim("yf", at["yf"])
                        products(down_ps[at["yf"] % 2][:, :], [(part(h_t, b, r, slice(i * P, (i + 1) * P)), part(wd, r))
                                                               for r in range(NR)]).then_inc(full["yf"], 1)

            run(pe, cnt, steps)

        wide = {"SPLIT_W0": (w0, w0_t[:, :, :]), "WO": (wo, raw_o)}

        def tile_halves(e, t):
            op, src = e[0], tr_ps[t % 2][:, :]
            if op == "CT":
                return part(ctx_t, e[1], e[2]), src
            if op == "XT":
                return [xt[:, k, e[1], e[2]] for k in range(2)], src
            if op == "AT":
                return part(att_t, e[2]), src
            if op == "TV":
                return part(v_s, e[1]), src.rearrange("p (i d) -> p i d", d=DH)
            return part(p_t, e[3] % 2), src

        def weight_halves(e):
            if e[0] == "WQKV":
                return [(wq, raw_q), (wk, raw_k), (wv, raw_v)]
            if e[0] == "WP":
                piece = e[1]
                k = 2 * (piece // 2) if piece < 4 else 2 * (piece - 4)
                w = (wg, wu)[piece % 2] if piece < 4 else wd
                src = raw[:, piece % 3, :]
                if piece < 4:
                    dst = [h[:, k:k + 2].rearrange("p k (r j) -> p k r j", r=NR) for h in w]
                    return [(dst, src.rearrange("p (k j r) -> p k r j", k=2, r=NR))]
                return [([h[:, k:k + 2] for h in w], src.rearrange("p (k n) -> p k n", k=2))]
            return [wide[e[0]]]

        @block.scalar
        def _(act):
            cnt = Counts(act, ("pj", "s", "t", "o", "y", "gu", "yf", "kept", "qkv", "wol", "piece0", "piece1", "piece2"))
            act.wait_ge(setup_landed, 16 * 6)
            nc.scalar.activation(w0_ste, w0_raw, ACT.Abs, accum_out=total).then_inc(ternary_done, 1)
            for m in range(2):
                act.wait_ge(setup_t, KD + m + 1)
                nc.scalar.activation(wqk0[:, 0, m], score_ps[m][:, 0:C].rearrange("p (c n) -> p c n", c=KC), ACT.Copy,
                                     scale=(-1.0, 1.0)[m]).then_inc(setup_hi, 1)
            late = []

            def absolutes():
                while late:
                    r, n = late.pop()
                    act.wait_ge(taken["gu"], cnt.value("gu", n + 1 + SLOTS["gu"]))
                    nc.scalar.activation(h_abs[:, r, :], h_f[:, r, :], ACT.Abs).then_inc(abs_done, 1)

            def steps(kind, order, pair):
                for e in order:
                    op, at = e[0], cnt.step(e)
                    if op in ("CT", "XT", "AT", "T", "TV"):
                        dst, src = tile_halves(e, at["t"])
                        act.wait_ge(full["t"], cnt.value("t", at["t"] + 1))
                        nc.scalar.activation(dst[0], src, ACT.Copy).then_inc(hi_done, 1)
                    elif op in ("K0", "Q0"):
                        act.wait_ge(full["pj"], cnt.value("pj", at["pj"] + 1))
                        dst, bias = (k_t[0][:, e[1]], bk) if op == "K0" else (q_t[0][:, e[1], 0], nbq)
                        nc.scalar.activation(dst, proj_ps[at["pj"] % 2][:, :], ACT.Identity, bias=bias)\
                            .then_inc(hi_done, 1)
                    elif op in ("K", "Q"):
                        act.wait_ge(full["pj"], cnt.value("pj", at["pj"] + 1))
                        dst, scale = (k_t[0][:, e[1]], 1.0) if op == "K" else (q_t[0][:, e[1], e[2]], -SCORE_SCALE)
                        nc.scalar.activation(dst, proj_ps[at["pj"] % 2][:, :], ACT.Copy, scale=scale).then_inc(hi_done, 1)
                    elif op in ("E", "S"):
                        u, i = (e[1], e[2]) if op == "E" else (e[2], e[3])
                        act.wait_ge(taken["s"], cnt.value("s", at["s"] + 1 + SLOTS["s"]))
                        nc.scalar.activation(prob[:, u, i, :], prob[:, u, i, :], ACT.Exp, bias=smin[:, u, i:i + 1],
                                             scale=-1.0, accum_out=ssum[:, u, i:i + 1]).then_inc(exp_done, 1)
                    elif op == "PV" and e[3] == NT - 1:
                        act.wait_ge(full["o"], cnt.value("o", at["o"] + 1))
                        nc.scalar.activation(o_t[0][:, e[1], e[2]], o_ps[:, :], ACT.Copy).then_inc(hi_done, 1)
                    elif op in ("SPLIT_W0", "WQKV", "WO", "WP"):
                        if op == "WQKV":
                            act.wait_ge(qkv_landed, cnt.value("qkv", at["qkv"] + 48))
                        elif op == "WO":
                            act.wait_ge(wo_landed, cnt.value("wol", at["wol"] + 16))
                            act.wait_ge(full["y"], cnt.value("y", cnt.n["y"]))
                        elif op == "WP":
                            slot = f"piece{e[1] % 3}"
                            act.wait_ge(mlp_landed[e[1] % 3], cnt.value(slot, at[slot] + 16))
                            if e[1] == 4 and "yf" in cnt.n:
                                act.wait_ge(full["yf"], cnt.value("yf", cnt.n["yf"]))
                        for dst, src in weight_halves(e):
                            nc.scalar.activation(dst[0], src, ACT.Copy).then_inc(hi_done, 1)
                    elif op == "GU":
                        b, r = e[1:]
                        act.wait_ge(full["gu"], cnt.value("gu", at["gu"] + 1))
                        nc.scalar.activation(silu[:, at["gu"] % 2, :], gate_ps[at["gu"] % 2][:, :], ACT.Silu)\
                            .then_inc(silu_done, 1)
                        absolutes()
                        late.append((r, at["gu"]))
                    elif op == "KEEP":
                        absolutes()
                        for r in range(NR):
                            act.wait_ge(kept_done, cnt.value("kept", at["kept"] + r + 1))
                            nc.scalar.activation(h_t[0][:, e[1], r], h_f[:, r, :], ACT.Copy).then_inc(hi_done, 1)

            run(act, cnt, steps)

        @block.vector
        def _(dve):
            cnt = Counts(dve, ("pj", "s", "t", "o", "y", "yf", "hi", "exp", "rstd", "sg", "ab", "hs", "step"))
            V = nc.vector

            def low(dst, src, n, bump, amount=1):
                dve.wait_ge(hi_done, cnt.value("hi", n + 1))
                V.tensor_tensor(dst[1], src, dst[0].bitcast(F32), ALU.subtract).then_inc(bump, amount)

            for k, (ring, slots) in enumerate(SLOTS.items()):
                V.memset(marks[:, k:k + 1], 0.0).then_inc(taken[ring], slots)
            V.memset(marks[:, 7 + 3:7 + 4], 0.0).then_inc(h_split, 1)
            dve.wait_ge(setup_sum, 1)
            V.tensor_scalar(scale0, y_ps[:, 0:1], 1.0 / (D * D), None, ALU.mult).then_inc(ternary_step, 1)
            dve.wait_ge(ternary_step, 1)
            V.tensor_scalar(cut, scale0, TERNARY_EPS, 0.5, ALU.add, ALU.mult).then_inc(ternary_step, 1)
            dve.wait_ge(ternary_step, 2)
            V.tensor_scalar(ncut, cut, -1.0, None, ALU.mult).then_inc(ternary_step, 1)
            V.tensor_scalar(nbq, small[:, 6:7], -1.0, None, ALU.mult)
            dve.wait_ge(ternary_step, 3)
            V.tensor_scalar(w0_ste, w0_raw, ncut, None, ALU.is_lt).then_inc(ternary_step, 1)
            dve.wait_ge(ternary_step, 4)
            V.scalar_tensor_tensor(w0_ste, w0_raw, cut, w0_ste, ALU.is_gt, ALU.subtract).then_inc(ternary_step, 1)
            dve.wait_ge(ternary_step, 5)
            V.scalar_tensor_tensor(w0_ste, w0_ste, scale0, w0_raw, ALU.mult, ALU.subtract).then_inc(ternary_step, 1)
            dve.wait_ge(ternary_step, 6)
            V.tensor_tensor(w0_ste, w0_ste, w0_raw, ALU.add).then_inc(ternary_done, 1)
            for j in range(KD):
                dve.wait_ge(setup_t, j + 1)
                V.tensor_copy(w0_t[:, j, :], tr_ps[j % 2][:, :]).then_inc(setup_taken, 1)
            for m in range(2):
                dve.wait_ge(setup_hi, m + 1)
                last = V.scalar_tensor_tensor(wqk0[:, 1, m], score_ps[m][:, 0:C].rearrange("p (c n) -> p c n", c=KC),
                                              (-1.0, 1.0)[m], wqk0[:, 0, m].bitcast(F32), ALU.mult, ALU.subtract)
            last.then_inc(phase_done, 1)

            def steps(kind, order, pair):
                for e in order:
                    op, at = e[0], cnt.step(e)
                    if op == "NO_MASK":
                        V.memset(mask_add[:, :, :], 0.0).then_inc(dve_step, 1)
                        dve.wait_ge(dve_step, cnt.value("step", at["step"] + 1))
                    elif op == "MASK":
                        dve.wait_ge(mask_landed, dve.snap(pair * 32) + 32)
                        V.tensor_scalar(mask_add[:, :, :], mask_u8[:, :, :], -MASKED, MASKED, ALU.mult, ALU.add)\
                            .then_inc(dve_step, 1)
                        V.tensor_reduce(any_valid[:, :], mask_u8[:, :, :], AX_X, ALU.max).then_inc(dve_step, 1)
                        dve.wait_ge(dve_step, cnt.value("step", at["step"] + 2))
                    elif op == "LN":
                        b = e[1]
                        if kind == "first" and cnt.n.get("y", 0) == 0:
                            dve.wait_ge(x_landed, dve.snap(pair * 16) + 16)
                        else:
                            dve.wait_ge(taken["y"], cnt.value("y", cnt.n["y"] + SLOTS["y"]))
                        for i in range(NT):
                            V.bn_stats(bn[:, i, :], x[:, b, i, :]).then_inc(dve_step, 1)
                        for i in range(NT):
                            dve.wait_ge(dve_step, cnt.value("step", at["step"] + i + 1))
                            stand(dve)
                            last = V.bn_aggr(mv[:, b, i, :], bn[:, i, :])
                        last.then_inc(stats_done, 1)
                        dve.wait_ge(rstd_done, cnt.value("rstd", at["rstd"] + 2))
                        for i in range(NT):
                            V.tensor_scalar(xn[:, b, i, :], x[:, b, i, :], mv[:, b, i, 0:1], rstd[:, b, i:i + 1],
                                            ALU.subtract, ALU.mult).then_inc(xn_done, 1)
                    elif op == "ADD_BIAS":
                        for b in range(2):
                            for i in range(NT):
                                last = V.tensor_tensor(x[:, b, i, :], x[:, b, i, :], bias0[:, :], ALU.add)
                        last.then_inc(dve_step, 1)
                        dve.wait_ge(dve_step, cnt.value("step", at["step"] + 1))
                    elif op in ("CT", "XT", "AT", "T", "TV"):
                        dst, src = tile_halves(e, at["t"])
                        low(dst, src, at["hi"], taken["t"])
                    elif op in ("K0", "Q0"):
                        dst, bias = (part(k_t, e[1]), bk) if op == "K0" else (part(q_t, e[1], 0), nbq)
                        dve.wait_ge(hi_done, cnt.value("hi", at["hi"] + 1))
                        V.scalar_tensor_tensor(dst[1], proj_ps[at["pj"] % 2][:, :], bias, dst[0].bitcast(F32),
                                               ALU.add, ALU.subtract).then_inc(taken["pj"], 1)
                    elif op == "K":
                        low(part(k_t, e[1]), proj_ps[at["pj"] % 2][:, :], at["hi"], taken["pj"])
                    elif op == "Q":
                        dst = part(q_t, e[1], e[2])
                        dve.wait_ge(hi_done, cnt.value("hi", at["hi"] + 1))
                        V.scalar_tensor_tensor(dst[1], proj_ps[at["pj"] % 2][:, :], -SCORE_SCALE, dst[0].bitcast(F32),
                                               ALU.mult, ALU.subtract).then_inc(taken["pj"], 1)
                    elif op == "VT":
                        dve.wait_ge(full["pj"], cnt.value("pj", at["pj"] + 1))
                        V.tensor_copy(v_tmp, proj_ps[at["pj"] % 2][:, :]).then_inc(taken["pj"], 1)
                    elif op in ("E", "S"):
                        b, u, i = (e[1], e[1], e[2]) if op == "E" else e[1:]
                        dve.wait_ge(full["s"], cnt.value("s", at["s"] + 1))
                        stand(dve)
                        V.tensor_tensor_reduce(out=prob[:, u, i, :], in0=score_ps[at["s"] % 2][:, :],
                                               in1=mask_add[:, b, :], scale=1.0, scalar=MIN_START, op0=ALU.add,
                                               op1=ALU.min, accum_out=smin[:, u, i:i + 1]).then_inc(taken["s"], 1)
                    elif op == "RS":
                        u = e[1]
                        dve.wait_ge(exp_done, cnt.value("exp", cnt.n["exp"]))
                        V.reciprocal(srec[:, u, :], ssum[:, u, :]).then_inc(rs_done, 1)
                    elif op == "PV" and e[3] == NT - 1:
                        low(part(o_t, e[1], e[2]), o_ps[:, :], at["hi"], taken["o"])
                    elif op in ("XM", "FC", "Y"):
                        b, i = e[1:]
                        dve.wait_ge(full["y"], cnt.value("y", at["y"] + 1))
                        V.tensor_tensor(x[:, b, i, :], y_ps[:, :], x[:, b, i, :], ALU.add).then_inc(taken["y"], 1)
                    elif op in ("SPLIT_W0", "WQKV", "WO", "WP"):
                        bump = mlp_w_split if op == "WP" else w_split
                        for k, (dst, src) in enumerate(weight_halves(e)):
                            low(dst, src, at["hi"] + k, bump)
                    elif op == "GU":
                        b, r = e[1:]
                        if r == 0:
                            dve.wait_ge(h_split, cnt.value("hs", cnt.n.get("hs", 0) + 1))
                        dve.wait_ge(silu_done, cnt.value("sg", at["sg"] + 1))
                        V.tensor_tensor(h_f[:, r, :], up_ps[at["gu"] % 2][:, :], silu[:, at["gu"] % 2, :], ALU.mult)\
                            .then_inc(taken["gu"], 1)
                    elif op == "KEEP":
                        keep_two_of_four(e[1], at)
                    elif op == "DN":
                        b, i = e[1:]
                        dve.wait_ge(full["yf"], cnt.value("yf", at["yf"] + 1))
                        V.tensor_tensor(x[:, b, i, :], down_ps[at["yf"] % 2][:, :], x[:, b, i, :], ALU.add)\
                            .then_inc(taken["yf"], 1)
                ends = ("first", "attention end", "mlp end")
                if kind in ends:
                    k = len(SLOTS) + ends.index(kind)
                    V.memset(marks[:, k:k + 1], 0.0).then_inc(phase_done, 1)

            def keep_two_of_four(b, at):
                c01, c02, c03, c12, c13, c23 = (flags[:, k, :] for k in range(6))
                t0, t1, t2, t3, t4, t5 = (flags[:, k, :] for k in range(6, 12))
                k0 = at["step"]

                def after(k):
                    dve.wait_ge(dve_step, cnt.value("step", k0 + k))

                def mark(ins):
                    ins.then_inc(dve_step, 1)

                dve.wait_ge(abs_done, cnt.value("ab", cnt.n["ab"]))
                mark(V.tensor_tensor(flags[:, 0:3, :], h_abs[:, 0:1, :].to_broadcast([P, 3, S]), h_abs[:, 1:4, :], ALU.is_ge))
                mark(V.tensor_tensor(flags[:, 3:5, :], h_abs[:, 1:2, :].to_broadcast([P, 2, S]), h_abs[:, 2:4, :], ALU.is_ge))
                mark(V.tensor_tensor(c23, h_abs[:, 2, :], h_abs[:, 3, :], ALU.is_ge))
                after(1)
                mark(V.tensor_tensor(t0, c01, c02, ALU.add))
                after(2)
                mark(V.tensor_tensor(t1, c12, c13, ALU.add))
                mark(V.tensor_tensor(t2, c02, c12, ALU.add))
                mark(V.tensor_tensor(t3, c03, c13, ALU.add))
                after(4)
                mark(V.tensor_tensor(t4, t0, c03, ALU.add))
                after(5)
                mark(V.tensor_tensor(t5, t1, c01, ALU.subtract))
                after(6)
                mark(V.tensor_tensor(c02, t2, c23, ALU.subtract))
                after(7)
                mark(V.tensor_tensor(c12, t3, c23, ALU.add))
                for r, (t, bound, test) in enumerate(((t4, 1.5, ALU.is_gt), (t5, 0.5, ALU.is_gt),
                                                      (c02, 0.5, ALU.is_lt), (c12, 1.5, ALU.is_lt))):
                    after(8 + r)
                    V.scalar_tensor_tensor(h_f[:, r, :], t, bound, h_f[:, r, :], test, ALU.mult).then_inc(kept_done, 1)
                for r in range(NR):
                    low(part(h_t, b, r), h_f[:, r, :], at["hi"] + r, h_split)

            run(dve, cnt, steps)
    return nc


_INS = ["x", "ctx_1024", "mask_BxS2_bf1", "L0_xattn_Wq", "L0_xattn_bq", "L0_xattn_Wk", "L0_xattn_bk", "L0_ffn_weight",
        "L0_ffn_bias", "L1_xattn_Wq", "L1_xattn_Wk", "L1_xattn_Wv", "L1_xattn_Wo", "L1_ffn_w_gate", "L1_ffn_w_up",
        "L1_ffn_w_down"]


def kernel(**inputs):
    import numpy as np
    import concourse.bacc as bacc
    from concourse.bass_utils import run_bass_kernel_spmd

    nc = bacc.Bacc("TRN2", target_bir_lowering=False, num_devices=1)
    arrays, args = {}, []
    for name in _INS:
        a = np.ascontiguousarray(inputs[name])
        if a.dtype == np.bool_:
            a = a.view(np.uint8)
        arrays[f"in_{name}"] = a
        args.append(nc.dram_tensor(f"in_{name}", a.shape, mybir.dt.from_np(a.dtype), kind="ExternalInput").ap())
    out = nc.dram_tensor("out", (B, S, D), F32, kind="ExternalOutput").ap()
    build(nc, *args, out)
    r = run_bass_kernel_spmd(nc, [arrays], core_ids=[0])
    return r.results[0]["out"]
```

```python
from contextlib import ExitStack

import concourse.bass as bass
from concourse import mybir

F32 = mybir.dt.float32
F32R = mybir.dt.float32r
BF16 = mybir.dt.bfloat16
U8 = mybir.dt.uint8
ALU = mybir.AluOpType
ACT = mybir.ActivationFunctionType
AX_X = mybir.AxisListType.X

P = 128
B, S, D, C = 4, 512, 512, 256
NT = S // P
KD, KC = D // P, C // P
GROUPS, HPG, DH = 8, 2, 128
HIDDEN, CHUNK = 2048, 512
CHUNKS, NR = HIDDEN // CHUNK, 4
PAIRS = B // 2
LN_EPS = 1e-5
TERNARY_EPS = 1e-10
SCORE_SCALE = float(DH) ** -0.5
MASKED = 3e38
MIN_START = 3.4e38
AREA = 92 * 256

def norm(b):
    return [("LN_STATS", b), ("LN", b)]


def scores(b, h):
    s, n = [("S", b, h, i) for i in range(NT)], [("RS", h, b, i) for i in range(NT)]
    return [s[0], s[1], s[2], n[0]], [s[3], n[1]], [n[2]], [n[3]]


def weave(b, h, g0, g1, g2, g3, g4):
    t, v = [("T", b, h, j) for j in range(NT)], [("PV", b, h, j) for j in range(NT)]
    return [t[0], t[1], *g0, v[0], t[2], *g1, v[1], t[3], *g2, v[2], *g3, v[3], *g4]


def first_layers_order():
    def ct(b):
        return [("CT", b, c) for c in range(KC)]

    def e(b):
        s, n = [("E", b, i) for i in range(NT)], [("RS", b, b, i) for i in range(NT)]
        return [s[0], s[1], s[2], n[0], s[3], n[1], n[2], n[3]]

    at = [[("AT", b, j) for j in range(NT)] for b in (0, 1)]
    xt = [[("XT", b, j) for j in range(KD)] for b in (0, 1)]
    xm = [[("XM", b, i) for i in range(NT)] for b in (0, 1)]
    fc = [[("FC", b, i) for i in range(NT)] for b in (0, 1)]
    s0, s1, s2, s3 = scores(0, 0)
    return [
        ("NO_MASK",), *ct(0), ("K0", 0), ("Q0", 0), *ct(1), *e(0), ("K0", 1), ("Q0", 1), *norm(0), ("SPLIT_W0",),
        *e(1), *at[0], *xt[0], *norm(1),
        xm[0][0], *at[1][0:2], xm[0][1], *at[1][2:4], xm[0][2], *xt[1][0:2], xm[0][3], *xt[1][2:4],
        xm[1][0], ("LN_STATS", 0), xm[1][1], ("LN", 0), ("ADD_BIAS", 0), xm[1][2], *xt[0][0:2], xm[1][3], *xt[0][2:4],
        ("LN_STATS", 1), fc[0][0], ("LN", 1), ("ADD_BIAS", 1), fc[0][1], *xt[1][0:2], fc[0][2], *xt[1][2:4], fc[0][3],
        fc[1][0], ("LN_STATS", 0), fc[1][1], ("LN", 0), ("MASK",), fc[1][2], *xt[0][0:2], fc[1][3],
        *load_qkv(), *xt[0][2:4], ("K", 0), ("LN_STATS", 1), ("VT", 0), ("Q", 0, 0), ("LN", 1), ("TV", 0), ("Q", 0, 1),
        *s0, *xt[1][0:2], *s1, *xt[1][2:4], *s2, *s3,
    ]


def load_qkv():
    return [("WK",), ("WV",), ("WQ", 0), ("WQ", 1)]


def head(b, h, ahead, g0, g1, g2, g3, g4):
    t, v = [("T", b, h, j) for j in range(NT)], [("PV", b, h, j) for j in range(NT)]
    s, n = [("S", *ahead, i) for i in range(NT)], [("RS", ahead[1], ahead[0], i) for i in range(NT)]
    return [t[0], s[0], t[1], s[1], *g0, v[0], t[2], n[0], s[2], *g1, v[1], t[3], n[1], s[3], *g2, n[2], v[2], n[3],
            *g3, v[3], *g4]


def group_order(first, last):
    y = [[("Y", b, i) for i in range(NT)] for b in (0, 1)]
    yp = [[]] * NT if first else [[t] for t in y[1]]
    k, v, q0, q1 = load_qkv()
    wkv, wq = ([], []) if last else ([k, v], [q0, q1])
    o = head(0, 0, (0, 1), [], [("K", 1)], [("VT", 1)], [("Q", 1, 0)], [("TV", 1), *yp[0], *wkv])
    o += head(0, 1, (1, 0), [], yp[1], yp[2], [("Q", 1, 1)], [*yp[3], ("WO", 0), ("WO", 1)])
    if not last:
        o += head(1, 0, (1, 1), wq, [("K", 0)], [y[0][0]], [("Q", 0, 0)], [y[0][1]])
        o += head(1, 1, (0, 0), [], [("VT", 0)], [y[0][2]], [("Q", 0, 1)], [("TV", 0), y[0][3]])
        return o
    a0, a1, a2, a3 = scores(1, 1)
    piece = [("WP", p) for p in range(6)]
    xt = [[("XT", b, j) for j in range(KD)] for b in (0, 1)]
    gu = [("GU", 0, r) for r in range(NR)]
    o += weave(1, 0, a0, [*a1, y[0][0], *a2], [*a3, y[0][1]], [piece[0], y[0][2]], [y[0][3], ("LN_STATS", 0)])
    o += weave(1, 1, [("LN", 0)], [piece[1]], [xt[0][0]], xt[0][1:3], [piece[2], xt[0][3]])
    o += [*y[1], piece[3], gu[0], ("LN_STATS", 1), ("LN", 1), *piece[4:], gu[1], *xt[1][0:2], gu[2], ("CMP", 0, 1),
          *xt[1][2:4], gu[3], ("CMP", 0, 2), ("KEEP", 0)]
    return o


def mlp_order(first, last):
    o = []
    for b in (0, 1):
        gu = [("GU", b, r) for r in range(NR)]
        if b or not first:
            o += [gu[0], *([("HALVES", 0)] if b else []), gu[1], gu[2], ("CMP", b, 1), gu[3], ("CMP", b, 2), ("KEEP", b)]
    piece = [[]] * 6 if last else [[("WP", p)] for p in range(6)]
    dn = [[("DN", b, i) for i in range(NT)] for b in (0, 1)]
    o += [("HALVES", 1), *piece[0], *piece[1], *piece[2], *dn[0], *piece[3], *dn[1], *piece[4], *piece[5]]
    return o


MOVES = {
    "NO_MASK": {"step": 1}, "MASK": {"step": 2}, "ADD_BIAS": {"step": 1},
    "LN_STATS": {"step": NT, "stat": 1, "rstd": 2}, "LN": {"xn": NT},
    "SPLIT_W0": {"hi": 1, "w": 1}, "WK": {"hi": 1, "w": 1, "qkv": 48}, "WV": {"hi": 1, "w": 1},
    "WQ": {"hi": 1, "w": 1},
    "CT": {"t": 1, "hi": 1}, "XT": {"t": 1, "hi": 1}, "AT": {"t": 1, "hi": 1}, "T": {"t": 1, "hi": 1},
    "TV": {"t": 1, "hi": 1}, "K0": {"pj": 1, "hi": 1}, "Q0": {"pj": 1, "hi": 1}, "K": {"pj": 1, "hi": 1},
    "Q": {"pj": 1, "hi": 1}, "VT": {"pj": 1}, "E": {"s": 1, "exp": 1}, "S": {"s": 1, "exp": 1},
    "RS": {"rs": 1, "norm": 1}, "XM": {"z": 1}, "FC": {"z": 1}, "Y": {"y": 1},
    "GU": {"gu": 1, "sg": 1, "ab": 1}, "KEEP": {"kept": NR, "step": 7}, "HALVES": {"hi": NR, "hs": NR},
    "DN": {"yf": 1},
}


def moves(e):
    if e[0] == "PV":
        return {"o": 1, "hi": 1} if e[3] == NT - 1 else {}
    if e[0] == "WO":
        return {"hi": 1, "w": 1, "wol": 16 * (e[1] == 0)}
    if e[0] == "CMP":
        return {"step": (1, 3)[e[2] - 1]}
    if e[0] == "WP":
        return {"fw": 1, "hi": 1, f"piece{e[1] % 3}": 16}
    return MOVES[e[0]]


def total_moves(order):
    out = {}
    for e in order:
        for k, v in moves(e).items():
            out[k] = out.get(k, 0) + v
    return out


class Counts:

    def __init__(self, eng, used):
        self.eng, self.used = eng, used
        self.n, self.past, self.base = {}, {}, {k: 0 for k in used}

    def step(self, e):
        at = {k: self.n.get(k, 0) for k in moves(e)}
        for k, v in moves(e).items():
            self.n[k] = at[k] + v
        return at

    def value(self, k, n):
        return self.base[k] + n

    def loop(self, reg, per):
        outer = dict(self.base)
        for k in self.used:
            if per.get(k):
                self.base[k] = self.eng.snap(reg * per[k] + self.base[k])
        return outer

    def after_loop(self, outer, per, trips):
        self.base = outer
        for k, v in per.items():
            self.past[k] = self.past.get(k, 0) + v * (trips - 1)
            if k in self.used:
                self.base[k] = self.eng.snap(outer[k] + v * (trips - 1))


PER_GROUP = total_moves(group_order(False, False))
PER_CHUNK = total_moves(mlp_order(False, False))
PER_PAIR = total_moves(first_layers_order() + group_order(True, False) + group_order(False, False) * (GROUPS - 2)
                       + group_order(False, True) + mlp_order(True, False) + mlp_order(False, False) * (CHUNKS - 2)
                       + mlp_order(False, True))


def build(nc, x_in, ctx_in, mask_in, wq0_in, bq0_in, wk0_in, bk0_in, w0_in, b0_in,
          wq_in, wk_in, wv_in, wo_in, wg_in, wu_in, wd_in, out):
    x_rows = x_in.rearrange("(q b) (i p) d -> q p b i d", b=2, p=P)
    out_rows = out.rearrange("(q b) (i p) d -> q p b i d", b=2, p=P)
    ctx_rows = ctx_in.rearrange("(q b) (i p) c -> q p b i c", b=2, p=P)
    mask_rows = mask_in.rearrange("(q b) s -> q b s", b=2)
    wq_cols = wq_in.rearrange("(k p) n -> p k n", p=P)
    wk_cols = wk_in.rearrange("(k p) n -> p k n", p=P)
    wv_cols = wv_in.rearrange("(k p) n -> p k n", p=P)
    wo_rows = wo_in.rearrange("(g h d) n -> g d h n", g=GROUPS, h=HPG)
    wg_cols = wg_in.rearrange("(k p) n -> p k n", p=P)
    wu_cols = wu_in.rearrange("(k p) n -> p k n", p=P)
    wd_rows = wd_in.rearrange("(c j r) n -> c j r n", c=CHUNKS, r=NR)

    with ExitStack() as es:
        def sb(name, shape, dt=F32):
            return es.enter_context(nc.sbuf_tensor(name, shape, dt))

        x = sb("x", [P, 2, NT, D])
        ident = sb("ident", [P, P])
        w0_t = sb("w0_t", [P, KD, D])
        bias0 = sb("bias0", [P, D])
        mask_add = sb("mask_add", [P, 2, S])
        mask_u8 = sb("mask_u8", [P, 2, S], U8)
        any_valid = sb("any_valid", [P, 2])
        small = sb("small", [P, 8])
        nbq, bk = small[:, 0:1], small[:, 1:2]
        total, scale0, cut, ncut = small[:, 2:3], small[:, 3:4], small[:, 4:5], small[:, 5:6]
        marks = sb("marks", [P, 16])
        ones = sb("ones", [P, P])
        half = sb("half", [P, NT])
        smin, ssum, srec = sb("smin", [P, 2, NT]), sb("ssum", [P, 2, NT]), sb("srec", [P, 2, NT])
        bn = sb("bn", [P, 2, NT, 6])
        mv = sb("mv", [P, 2, NT, 2])
        rstd = sb("rstd", [P, 2, NT])
        xn = sb("xn", [P, 2, NT, D])
        prob = sb("prob", [P, 2, NT, S])
        raw = sb("raw", [P, 3, 2 * D])
        v_tmp = sb("v_tmp", [P, S])
        xt = sb("xt", [P, 2, 2, KD, S], F32R)
        wqk0 = sb("wqk0", [P, 2, 2, KC, P], F32R)
        area = sb("area", [P, AREA], F32R)

        def half_views(at, *shape):
            n = 1
            for m in shape:
                n *= m
            names = "abcd"[:len(shape)]
            out = []
            for k in range(2):
                v = area[:, at + k * n:at + (k + 1) * n]
                if len(shape) > 1:
                    v = v.rearrange(f"p ({' '.join(names)}) -> p {' '.join(names)}", **dict(zip(names, shape)))
                out.append(v)
            return out, at + 2 * n

        ctx_t, at = half_views(0, 2, KC, S)
        wq, at = half_views(at, KD, HPG * DH)
        wk, at = half_views(at, KC, DH)
        wv, at = half_views(at, KC, DH)
        q_t, at = half_views(at, 2, HPG, S)
        k_t, at = half_views(at, 2, S)
        w0_at = at
        v_s, at = half_views(at, 2, NT, DH)
        p_t, at = half_views(at, 2, S)
        att_at = at
        o_t, at = half_views(at, 2, HPG, S)
        wo, at = half_views(at, HPG, D)
        assert at <= AREA
        w0, _ = half_views(w0_at, KD, D)
        att_t = [half_views(att_at, NT, S)[0], half_views(2 * 2 * KC * S, NT, S)[0]]
        wg, at = half_views(0, KD, CHUNK)
        wu, at = half_views(at, KD, CHUNK)
        wd, at = half_views(at, NR, D)
        h_t, at = half_views(at, 2, NR, S)
        assert at <= AREA
        ctx_raw = prob[:, 0, :, :].rearrange("p i d -> p (i d)").rearrange("p (b i c) -> p b i c", b=2, i=NT)
        raw_flat = raw[:, :, :].rearrange("p a n -> p (a n)")
        nq, nk = KD * HPG * DH, KC * DH
        raw_q = raw_flat[:, 0:nq].rearrange("p (k n) -> p k n", k=KD)
        raw_k = raw_flat[:, nq:nq + nk].rearrange("p (k n) -> p k n", k=KC)
        raw_v = raw_flat[:, nq + nk:nq + 2 * nk].rearrange("p (k n) -> p k n", k=KC)
        raw_o = raw_flat[:, nq + 2 * nk:nq + 2 * nk + HPG * D].rearrange("p (h n) -> p h n", h=HPG)
        w0_raw = xn[:, 0]
        w0_ste = xn[:, 1]
        wqk0_raw = prob[:, 1, 0:2, 0:C]
        h_f, h_abs = prob[:, 0], prob[:, 1]
        silu = xn[:, 0, 0:2]
        flags = xn[:, :, :, :].rearrange("p a i d -> p (a i d)")[:, 1024:].bitcast(BF16)\
            .rearrange("p (c n) -> p c n", n=S)

        bank = [es.enter_context(nc.psum_tensor(f"bank{i}", [P, 512], F32)) for i in range(8)]
        proj_ps, score_ps, tr_ps, o_ps, y_ps = bank[0:2], bank[2:4], bank[4:6], bank[6], bank[7]
        gate_ps, up_ps = bank[2:4], bank[0:2]
        RINGS = {"pj": (0, 1), "s": (2, 3), "t": (4, 5), "o": (6,), "y": (7,), "z": (7, 6, 2, 3), "gu": (0, 1),
                 "yf": (6, 7, 4, 5)}

        def sem(name):
            return es.enter_context(nc.semaphore(name))

        full = {k: sem(f"{k}_full") for k in RINGS}
        taken = {k: sem(f"{k}_taken") for k in RINGS}
        SLOTS = {k: len(v) for k, v in RINGS.items()}
        hi_done, exp_done, rs_done, norm_done = sem("hi_done"), sem("exp_done"), sem("rs_done"), sem("norm_done")
        stats_done, rstd_done, xn_done = sem("stats_done"), sem("rstd_done"), sem("xn_done")
        silu_done, abs_done, kept_done, h_split = sem("silu_done"), sem("abs_done"), sem("kept_done"), sem("h_split")
        w_split, mlp_w_split = sem("w_split"), sem("mlp_w_split")
        x_landed, ctx_landed, mask_landed = [sem("x_landed0"), sem("x_landed1")], sem("ctx_landed"), sem("mask_landed")
        qkv_landed, wo_landed = sem("qkv_landed"), sem("wo_landed")
        mlp_landed = [sem(f"mlp_landed{i}") for i in range(3)]
        stored, setup_landed, setup_done = [sem("stored0"), sem("stored1")], sem("setup_landed"), sem("setup_done")
        ident_done, ternary_done, ternary_step, setup_sum, setup_t, setup_taken, setup_hi, dve_step = (
            sem("ident_done"), sem("ternary_done"), sem("ternary_step"), sem("setup_sum"), sem("setup_t"), sem("setup_taken"),
            sem("setup_hi"), sem("dve_step"))

        def run(eng, cnt, steps):
            with eng.Fori(0, PAIRS) as pair:
                outer = cnt.loop(pair, PER_PAIR)
                steps(first_layers_order() + group_order(True, False), pair)
                with eng.Fori(1, GROUPS - 1) as g:
                    before = cnt.loop(eng.snap(g - 1), PER_GROUP)
                    steps(group_order(False, False), pair)
                cnt.after_loop(before, PER_GROUP, GROUPS - 2)
                steps(group_order(False, True) + mlp_order(True, False), pair)
                with eng.Fori(1, CHUNKS - 1) as c:
                    before = cnt.loop(eng.snap(c - 1), PER_CHUNK)
                    steps(mlp_order(False, False), pair)
                cnt.after_loop(before, PER_CHUNK, CHUNKS - 2)
                steps(mlp_order(False, True), pair)
                assert all(cnt.n[k] + cnt.past.get(k, 0) == v for k, v in PER_PAIR.items())
            cnt.base = outer

        WEIGHTS = ("SPLIT_W0", "WK", "WV", "WQ", "WO", "WP")

        def weight_halves(e):
            op = e[0]
            if op == "SPLIT_W0":
                return w0, w0_t[:, :, :]
            if op == "WK":
                return wk, raw_k
            if op == "WV":
                return wv, raw_v
            if op == "WQ":
                k = slice(2 * e[1], 2 * e[1] + 2)
                return part(wq, k), raw_q[:, k]
            if op == "WO":
                return part(wo, e[1]), raw_o[:, e[1]]
            piece, src = e[1], raw[:, e[1] % 3, :]
            if piece < 4:
                k = 2 * (piece // 2)
                dst = [h.rearrange("p k (r j) -> p k r j", r=NR) for h in part((wg, wu)[piece % 2], slice(k, k + 2))]
                return dst, src.rearrange("p (k j r) -> p k r j", k=2, r=NR)
            k = 2 * (piece - 4)
            return part(wd, slice(k, k + 2)), src.rearrange("p (k n) -> p k n", k=2)

        def part(halves, *ix):
            return [v[(slice(None), *ix)] for v in halves]

        def stand(eng):
            eng.nop(nofuse=True)

        block = es.enter_context(nc.Block())

        @block.sync
        def _(sp):
            sp.dma_start(w0_raw, w0_in.rearrange("(a p) n -> p a n", p=P)).then_inc(setup_landed, 16)
            sp.dma_start(wqk0_raw[:, 0], wq0_in).then_inc(setup_landed, 16)
            sp.dma_start(wqk0_raw[:, 1], wk0_in).then_inc(setup_landed, 16)
            sp.dma_start(bias0[:, :], b0_in.rearrange("(a n) -> a n", a=1).to_broadcast([P, D])).then_inc(setup_landed, 16)
            sp.dma_start(small[:, 6:7], bq0_in.rearrange("(p a) -> p a", a=1)).then_inc(setup_landed, 16)
            sp.dma_start(bk, bk0_in.rearrange("(p a) -> p a", a=1)).then_inc(setup_landed, 16)

            with sp.Fori(0, PAIRS) as pair:
                w_base = sp.snap(pair * PER_PAIR["w"])
                fw_base = sp.snap(pair * PER_PAIR["fw"])
                for b in range(2):
                    sp.wait_ge(stored[b], sp.snap(pair * 16) + 16)
                    stand(sp)
                    sp.dma_start(x[:, b], x_rows[bass.ds(pair, 1)][0][:, b]).then_inc(x_landed[b], 16)
                sp.wait_ge(mlp_w_split, fw_base + 1)
                stand(sp)
                for b in range(2):
                    sp.dma_start(mask_u8[:, b, :], mask_rows[bass.ds(pair, 1), b, :].to_broadcast([P, S]))\
                        .then_inc(mask_landed, 16)

                def load_qkv(g):
                    sp.dma_start(raw_k, wk_cols[:, :, bass.ds(g * DH, DH)]).then_inc(qkv_landed, 16)
                    sp.dma_start(raw_v, wv_cols[:, :, bass.ds(g * DH, DH)]).then_inc(qkv_landed, 16)
                    sp.dma_start(raw_q, wq_cols[:, :, bass.ds(g * (HPG * DH), HPG * DH)]).then_inc(qkv_landed, 16)

                def load_wo(g):
                    sp.dma_start(raw_o, wo_rows[bass.ds(g, 1)][0]).then_inc(wo_landed, 16)

                load_qkv(0)
                load_wo(0)
                with sp.Fori(1, GROUPS) as g:
                    split = sp.snap(g * 6 + w_base)
                    sp.wait_ge(w_split, split)
                    stand(sp)
                    load_qkv(g)
                    sp.wait_ge(w_split, split + 4)
                    stand(sp)
                    load_wo(g)

                def load_piece(piece, c):
                    dst = raw[:, piece % 3, :].rearrange("p (k n) -> p k n", k=2)
                    if piece < 4:
                        src = (wg_cols, wu_cols)[piece % 2][:, 2 * (piece // 2):2 * (piece // 2) + 2,
                                                            bass.ds(c * CHUNK, CHUNK)]
                    else:
                        src = wd_rows[bass.ds(c, 1)][0][:, 2 * (piece - 4):2 * (piece - 4) + 2, :]
                    sp.dma_start(dst, src).then_inc(mlp_landed[piece % 3], 16)

                sp.wait_ge(w_split, w_base + PER_PAIR["w"] + 1)
                stand(sp)
                for piece in range(3):
                    load_piece(piece, 0)
                for piece in range(3, 6):
                    sp.wait_ge(mlp_w_split, fw_base + (piece - 1))
                    stand(sp)
                    load_piece(piece, 0)
                with sp.Fori(1, CHUNKS) as c:
                    split = sp.snap(c * 6 + fw_base)
                    for piece in range(6):
                        sp.wait_ge(mlp_w_split, split + (piece - 1))
                        stand(sp)
                        load_piece(piece, c)
                sums = sp.snap(pair * PER_PAIR["yf"] + (PER_PAIR["yf"] + SLOTS["yf"]))
                for b in range(2):
                    sp.wait_ge(taken["yf"], sums - NT * (1 - b))
                    stand(sp)
                    sp.dma_start(out_rows[bass.ds(pair, 1)][0][:, b], x[:, b]).then_inc(stored[b], 16)
            for b in range(2):
                sp.wait_ge(stored[b], 16 * PAIRS + 16)

        @block.gpsimd
        def _(pool):
            pool.memset(ident[:, :], 0.0).then_inc(ident_done, 1)
            pool.memset(ones[:, :], 1.0).then_inc(ident_done, 1)
            pool.memset(half[:, :], -0.5).then_inc(ident_done, 1)
            pool.wait_ge(ident_done, 3)
            pool.affine_select(out=ident[:, :], in_=ident[:, :], compare_op=ALU.not_equal, fill=1.0, base=0,
                               pattern=[[-1, P]], channel_multiplier=1).then_inc(ident_done, 1)
            cnt = Counts(pool, ("stat", "rstd", "rs", "hi", "hs"))

            def steps(order, pair):
                if order[0][0] == "NO_MASK":
                    pool.wait_ge(h_split, cnt.value("hs", NR))
                    stand(pool)
                    pool.dma_start(ctx_raw, ctx_rows[bass.ds(pair, 1)][0]).then_inc(ctx_landed, 16)
                for e in order:
                    op, at = e[0], cnt.step(e)
                    if op == "LN_STATS":
                        b = e[1]
                        pool.wait_ge(stats_done, cnt.value("stat", at["stat"] + 1))
                        stand(pool)
                        pool.tensor_scalar(rstd[:, b], mv[:, b, :, 1], LN_EPS, None, ALU.add).then_inc(rstd_done, 1)
                        pool.wait_ge(rstd_done, cnt.value("rstd", at["rstd"] + 1))
                        pool.tensor_tensor(rstd[:, b], rstd[:, b], half[:, :], ALU.pow).then_inc(rstd_done, 1)
                    elif op == "RS":
                        u, b, i = e[1:]
                        pool.wait_ge(rs_done, cnt.value("rs", at["rs"] + 1))
                        stand(pool)
                        pool.tensor_scalar(prob[:, u, i, :], prob[:, u, i, :], srec[:, u, i:i + 1],
                                           any_valid[:, b:b + 1], ALU.mult, ALU.mult).then_inc(norm_done, 1)
                    elif op in WEIGHTS:
                        dst, src = weight_halves(e)
                        pool.wait_ge(hi_done, cnt.value("hi", at["hi"] + 1))
                        pool.tensor_tensor(dst[1], src, dst[0].bitcast(F32), ALU.subtract)\
                            .then_inc(mlp_w_split if op == "WP" else w_split, 1)
                    elif op == "HALVES":
                        for r in range(NR):
                            pool.wait_ge(hi_done, cnt.value("hi", at["hi"] + r + 1))
                            pool.tensor_tensor(h_t[1][:, e[1], r], h_f[:, r, :], h_t[0][:, e[1], r].bitcast(F32),
                                               ALU.subtract).then_inc(h_split, 1)

            pool.wait_ge(setup_done, 1)
            run(pool, cnt, steps)

        def three(a, b):
            return ((a[0], b[0]), (a[0], b[1]), (a[1], b[0]))

        @block.tensor
        def _(pe):
            cnt = Counts(pe, ("pj", "s", "t", "o", "y", "z", "gu", "yf", "norm", "xn", "w", "fw", "hs"))
            user = {b: "gu" for b in range(4)} | {b: "yf" for b in range(4, 8)}
            made = {}

            def claim(ring, n):
                at = n % SLOTS[ring]
                for b in (RINGS[ring][at], *([2 + at] if ring == "gu" else [])):
                    if user[b] != ring:
                        pe.wait_ge(taken[user[b]], cnt.value(user[b], cnt.n.get(user[b], 0) + SLOTS[user[b]]))
                        user[b] = ring
                pe.wait_ge(taken[ring], cnt.value(ring, n + 1))

            def ready(ring, n):
                pe.wait_ge(taken[ring], cnt.value(ring, n + 1 + SLOTS[ring]))

            def products(dst, pairs):
                ops = [h for a, b in pairs for h in three(a, b)]
                for i, (w, m) in enumerate(ops):
                    last = nc.tensor.matmul(dst, w, m, start=i == 0, stop=i == len(ops) - 1)
                return last

            xt_b = [[xt[:, k, b] for k in range(2)] for b in range(2)]
            wq0t = [wqk0[:, k, 0] for k in range(2)]
            wk0t = [wqk0[:, k, 1] for k in range(2)]

            pe.wait_ge(ident_done, 4)
            pe.wait_ge(ternary_done, 1)
            nc.tensor.matmul(y_ps[:, 0:1], ones[:, :], total, start=True, stop=True).then_inc(setup_sum, 1)
            pe.wait_ge(ternary_done, 2)
            for j in range(KD):
                if j >= 2:
                    pe.wait_ge(setup_taken, j - 1)
                for i in range(KD):
                    last = nc.tensor.transpose(tr_ps[j % 2][:, i * P:(i + 1) * P], w0_ste[:, i, j * P:(j + 1) * P],
                                               ident[:, :])
                last.then_inc(setup_t, 1)
            for m in range(2):
                for c in range(KC):
                    last = nc.tensor.transpose(score_ps[m][:, c * P:(c + 1) * P], wqk0_raw[:, m, c * P:(c + 1) * P],
                                               ident[:, :])
                last.then_inc(setup_t, 1)

            def transpose4(n, src):
                for i in range(NT):
                    last = nc.tensor.transpose(tr_ps[n % 2][:, i * P:(i + 1) * P], src(i), ident[:, :])
                last.then_inc(full["t"], 1)

            def steps(order, pair):
                for e in order:
                    op, at = e[0], cnt.step(e)
                    if op == "CT":
                        b, c = e[1:]
                        if (b, c) == (0, 0):
                            pe.wait_ge(ctx_landed, pe.snap(pair * 16) + 16)
                        claim("t", at["t"])
                        transpose4(at["t"], lambda i: ctx_raw[:, b, i, c * P:(c + 1) * P])
                        made["ct", b] = at["t"]
                    elif op in ("K0", "Q0"):
                        b = e[1]
                        ready("t", made["ct", b])
                        claim("pj", at["pj"])
                        w = wk0t if op == "K0" else wq0t
                        products(proj_ps[at["pj"] % 2][:, :], [(part(w, c), part(ctx_t, b, c)) for c in range(KC)])\
                            .then_inc(full["pj"], 1)
                        made["q", b, 0] = at["pj"]
                    elif op in ("E", "S"):
                        b, h, i = e[1:] if op == "S" else (e[1], 0, e[2])
                        if i == 0:
                            ready("pj", made["q", b, h])
                        claim("s", at["s"])
                        products(score_ps[at["s"] % 2][:, :], [(part(q_t, b, h, slice(i * P, (i + 1) * P)), part(k_t, b))])\
                            .then_inc(full["s"], 1)
                    elif op == "LN":
                        made["xn", e[1]] = at["xn"] + NT
                    elif op == "SPLIT_W0":
                        made["w0"] = at["w"] + 1
                    elif op == "XT":
                        b, j = e[1:]
                        if j == 0:
                            pe.wait_ge(xn_done, cnt.value("xn", made["xn", b]))
                        claim("t", at["t"])
                        transpose4(at["t"], lambda i: xn[:, b, i, j * P:(j + 1) * P])
                        made["xt", b] = at["t"]
                    elif op == "RS":
                        made["norm", e[1]] = at["norm"] + 1
                    elif op in ("AT", "T"):
                        u, j = (e[1], e[2]) if op == "AT" else (e[2], e[3])
                        if j == 0:
                            pe.wait_ge(norm_done, cnt.value("norm", made["norm", u]))
                        claim("t", at["t"])
                        transpose4(at["t"], lambda i: prob[:, u, i, j * P:(j + 1) * P])
                        made["t", j] = at["t"]
                        if op == "AT":
                            made["at", u] = at["t"]
                    elif op == "XM":
                        b, i = e[1:]
                        if i == 0:
                            ready("t", made["at", b])
                            ready("t", made["xt", b])
                        claim("z", at["z"])
                        products(bank[RINGS["z"][at["z"] % 4]][:, :],
                                 [(part(xt_b[b], j, slice(i * P, (i + 1) * P)), part(att_t[b], j)) for j in range(NT)])\
                            .then_inc(full["z"], 1)
                    elif op == "FC":
                        b, i = e[1:]
                        if i == 0:
                            ready("t", made["xt", b])
                            pe.wait_ge(w_split, cnt.value("w", made["w0"] + 1))
                        claim("z", at["z"])
                        products(bank[RINGS["z"][at["z"] % 4]][:, :],
                                 [(part(xt_b[b], j, slice(i * P, (i + 1) * P)), part(w0, j)) for j in range(KD)])\
                            .then_inc(full["z"], 1)
                    elif op in ("WK", "WV", "WQ"):
                        made[op] = at["w"] + 1
                    elif op == "WO":
                        made["wo"] = at["w"] + 1
                    elif op in ("K", "VT", "Q"):
                        b = e[1]
                        if b == 0:
                            pe.wait_ge(w_split, cnt.value("w", made["W" + op[0]] + 1))
                        if op == "Q" and e[2] == 0:
                            ready("t", made["xt", b])
                        claim("pj", at["pj"])
                        made[e] = at["pj"]
                        if op == "Q":
                            h = e[2]
                            args = [(part(wq, k, slice(h * DH, (h + 1) * DH)), part(xt_b[b], k)) for k in range(KD)]
                            made["q", b, h] = at["pj"]
                        else:
                            args = [(part(wk if op == "K" else wv, c), part(ctx_t, b, c)) for c in range(KC)]
                        products(proj_ps[at["pj"] % 2][:, :], args).then_inc(full["pj"], 1)
                    elif op == "TV":
                        ready("pj", made["VT", e[1]])
                        claim("t", at["t"])
                        transpose4(at["t"], lambda i: v_tmp[:, i * P:(i + 1) * P])
                    elif op == "PV":
                        b, h, j = e[1:]
                        if j == 0:
                            claim("o", cnt.n.get("o", 0))
                        ready("t", made["t", j])
                        ops = three(part(v_s, b, j), part(p_t, j % 2))
                        for k, (w, m) in enumerate(ops):
                            last = nc.tensor.matmul(o_ps[:, :], w, m, start=(j, k) == (0, 0), stop=(j, k) == (NT - 1, 2))
                        if j == NT - 1:
                            last.then_inc(full["o"], 1)
                            made["o", b] = at["o"]
                    elif op == "Y":
                        b, i = e[1:]
                        if i == 0:
                            ready("o", made["o", b])
                            pe.wait_ge(w_split, cnt.value("w", made["wo"] + 1))
                        claim("y", at["y"])
                        products(y_ps[:, :], [(part(o_t, b, h, slice(i * P, (i + 1) * P)), part(wo, h))
                                              for h in range(HPG)]).then_inc(full["y"], 1)
                    elif op == "WP":
                        made["piece", e[1]] = at["fw"] + 1
                    elif op == "GU":
                        b, r = e[1:]
                        if r == 0:
                            pe.wait_ge(mlp_w_split, cnt.value("fw", made["piece", 3] + 1))
                            ready("t", made["xt", b])
                        claim("gu", at["gu"])
                        cols = slice(r * P, (r + 1) * P)
                        products(gate_ps[at["gu"] % 2][:, :], [(part(wg, k, cols), part(xt_b[b], k)) for k in range(KD)])
                        products(up_ps[at["gu"] % 2][:, :], [(part(wu, k, cols), part(xt_b[b], k)) for k in range(KD)])\
                            .then_inc(full["gu"], 1)
                    elif op == "HALVES":
                        made["h", e[1]] = at["hs"] + NR
                    elif op == "DN":
                        b, i = e[1:]
                        if (b, i) == (0, 0):
                            pe.wait_ge(mlp_w_split, cnt.value("fw", made["piece", 5] + 1))
                        if i == 0:
                            pe.wait_ge(h_split, cnt.value("hs", made["h", b] + NR))
                        claim("yf", at["yf"])
                        products(bank[RINGS["yf"][at["yf"] % 4]][:, :], [(part(h_t, b, r, slice(i * P, (i + 1) * P)), part(wd, r))
                                                               for r in range(NR)]).then_inc(full["yf"], 1)

            pe.wait_ge(setup_done, 1)
            run(pe, cnt, steps)

        def tile_halves(e, t):
            op, src = e[0], tr_ps[t % 2][:, :]
            if op == "CT":
                return part(ctx_t, e[1], e[2]), src
            if op == "XT":
                return [xt[:, k, e[1], e[2]] for k in range(2)], src
            if op == "AT":
                return part(att_t[e[1]], e[2]), src
            if op == "TV":
                return part(v_s, e[1]), src.rearrange("p (i d) -> p i d", d=DH)
            return part(p_t, e[3] % 2), src

        @block.scalar
        def _(act):
            cnt = Counts(act, ("pj", "s", "t", "o", "y", "gu", "yf", "xn", "kept", "qkv", "wol", "piece0", "piece1", "piece2"))
            act.wait_ge(setup_landed, 16 * 6)
            nc.scalar.activation(w0_ste, w0_raw, ACT.Abs, accum_out=total).then_inc(ternary_done, 1)
            for m in range(2):
                act.wait_ge(setup_t, KD + m + 1)
                nc.scalar.activation(wqk0[:, 0, m], score_ps[m][:, 0:C].rearrange("p (c n) -> p c n", c=KC), ACT.Copy,
                                     scale=(-1.0, 1.0)[m]).then_inc(setup_hi, 1)
            late = []

            made = {}
            scored = []

            def exps():
                while scored:
                    u, i, n = scored.pop()
                    act.wait_ge(taken["s"], cnt.value("s", n + 1 + SLOTS["s"]))
                    nc.scalar.activation(prob[:, u, i, :], prob[:, u, i, :], ACT.Exp, bias=smin[:, u, i:i + 1],
                                         scale=-1.0, accum_out=ssum[:, u, i:i + 1]).then_inc(exp_done, 1)

            def absolutes():
                while late:
                    r, n = late.pop()
                    act.wait_ge(taken["gu"], cnt.value("gu", n + 1 + SLOTS["gu"]))
                    nc.scalar.activation(h_abs[:, r, :], h_f[:, r, :], ACT.Abs).then_inc(abs_done, 1)

            def steps(order, pair):
                for e in order:
                    op, at = e[0], cnt.step(e)
                    waiting = len(scored)
                    if op in ("CT", "XT", "AT", "T", "TV"):
                        dst, src = tile_halves(e, at["t"])
                        act.wait_ge(full["t"], cnt.value("t", at["t"] + 1))
                        nc.scalar.activation(dst[0], src, ACT.Copy).then_inc(hi_done, 1)
                    elif op in ("K0", "Q0"):
                        act.wait_ge(full["pj"], cnt.value("pj", at["pj"] + 1))
                        dst, bias = (k_t[0][:, e[1]], bk) if op == "K0" else (q_t[0][:, e[1], 0], nbq)
                        nc.scalar.activation(dst, proj_ps[at["pj"] % 2][:, :], ACT.Identity, bias=bias)\
                            .then_inc(hi_done, 1)
                    elif op in ("K", "Q"):
                        act.wait_ge(full["pj"], cnt.value("pj", at["pj"] + 1))
                        dst, scale = (k_t[0][:, e[1]], 1.0) if op == "K" else (q_t[0][:, e[1], e[2]], -SCORE_SCALE)
                        nc.scalar.activation(dst, proj_ps[at["pj"] % 2][:, :], ACT.Copy, scale=scale).then_inc(hi_done, 1)
                    elif op in ("E", "S"):
                        exps()
                        scored.append((e[1], e[2], at["s"]) if op == "E" else (e[2], e[3], at["s"]))
                    elif op == "PV" and e[3] == NT - 1:
                        act.wait_ge(full["o"], cnt.value("o", at["o"] + 1))
                        nc.scalar.activation(o_t[0][:, e[1], e[2]], o_ps[:, :], ACT.Copy).then_inc(hi_done, 1)
                    elif op in WEIGHTS:
                        if op == "WK":
                            act.wait_ge(qkv_landed, cnt.value("qkv", at["qkv"] + 48))
                        elif op == "WO" and e[1] == 0:
                            act.wait_ge(wo_landed, cnt.value("wol", at["wol"] + 16))
                            act.wait_ge(full["y"], cnt.value("y", cnt.n.get("y", 0)))
                        elif op == "WP":
                            slot = f"piece{e[1] % 3}"
                            act.wait_ge(mlp_landed[e[1] % 3], cnt.value(slot, at[slot] + 16))
                            if e[1] == 4 and cnt.n.get("yf"):
                                act.wait_ge(full["yf"], cnt.value("yf", cnt.n["yf"]))
                        dst, src = weight_halves(e)
                        nc.scalar.activation(dst[0], src, ACT.Copy).then_inc(hi_done, 1)
                    elif op == "GU":
                        b, r = e[1:]
                        act.wait_ge(full["gu"], cnt.value("gu", at["gu"] + 1))
                        nc.scalar.activation(silu[:, at["gu"] % 2, :], gate_ps[at["gu"] % 2][:, :], ACT.Silu)\
                            .then_inc(silu_done, 1)
                        absolutes()
                        late.append((r, at["gu"]))
                    elif op == "KEEP":
                        absolutes()
                    elif op == "HALVES":
                        for r in range(NR):
                            act.wait_ge(kept_done, cnt.value("kept", made["kept", e[1]] + (1, 2, 4, 3)[r]))
                            nc.scalar.activation(h_t[0][:, e[1], r], h_f[:, r, :], ACT.Copy).then_inc(hi_done, 1)
                    if op == "KEEP":
                        made["kept", e[1]] = at["kept"]
                    if waiting and op not in ("E", "S", "RS"):
                        exps()
                exps()

            act.wait_ge(setup_done, 1)
            run(act, cnt, steps)

        @block.vector
        def _(dve):
            cnt = Counts(dve, ("pj", "s", "t", "o", "y", "z", "yf", "hi", "exp", "rstd", "xn", "sg", "ab", "hs", "step"))
            made = {}
            V = nc.vector

            def low(dst, src, n, bump, amount=1):
                dve.wait_ge(hi_done, cnt.value("hi", n + 1))
                V.tensor_tensor(dst[1], src, dst[0].bitcast(F32), ALU.subtract).then_inc(bump, amount)

            for k, (ring, slots) in enumerate(SLOTS.items()):
                V.memset(marks[:, k:k + 1], 0.0).then_inc(taken[ring], slots)
            V.memset(marks[:, 8:9], 0.0).then_inc(h_split, NR)
            for b in range(2):
                V.memset(marks[:, 12 + b:13 + b], 0.0).then_inc(stored[b], 16)
            V.memset(marks[:, 10:11], 0.0).then_inc(w_split, 1)
            V.memset(marks[:, 11:12], 0.0).then_inc(mlp_w_split, 1)
            dve.wait_ge(setup_sum, 1)
            V.tensor_scalar(scale0, y_ps[:, 0:1], 1.0 / (D * D), None, ALU.mult).then_inc(ternary_step, 1)
            dve.wait_ge(ternary_step, 1)
            V.tensor_scalar(cut, scale0, TERNARY_EPS, 0.5, ALU.add, ALU.mult).then_inc(ternary_step, 1)
            dve.wait_ge(ternary_step, 2)
            V.tensor_scalar(ncut, cut, -1.0, None, ALU.mult).then_inc(ternary_step, 1)
            V.tensor_scalar(nbq, small[:, 6:7], -1.0, None, ALU.mult)
            dve.wait_ge(ternary_step, 3)
            V.tensor_scalar(w0_ste, w0_raw, ncut, None, ALU.is_lt).then_inc(ternary_step, 1)
            dve.wait_ge(ternary_step, 4)
            V.scalar_tensor_tensor(w0_ste, w0_raw, cut, w0_ste, ALU.is_gt, ALU.subtract).then_inc(ternary_step, 1)
            dve.wait_ge(ternary_step, 5)
            V.scalar_tensor_tensor(w0_ste, w0_ste, scale0, w0_raw, ALU.mult, ALU.subtract).then_inc(ternary_step, 1)
            dve.wait_ge(ternary_step, 6)
            V.tensor_tensor(w0_ste, w0_ste, w0_raw, ALU.add).then_inc(ternary_done, 1)
            for j in range(KD):
                dve.wait_ge(setup_t, j + 1)
                V.tensor_copy(w0_t[:, j, :], tr_ps[j % 2][:, :]).then_inc(setup_taken, 1)
            for m in range(2):
                dve.wait_ge(setup_hi, m + 1)
                last = V.scalar_tensor_tensor(wqk0[:, 1, m], score_ps[m][:, 0:C].rearrange("p (c n) -> p c n", c=KC),
                                              (-1.0, 1.0)[m], wqk0[:, 0, m].bitcast(F32), ALU.mult, ALU.subtract)
            last.then_inc(setup_done, 1)
            dve.wait_ge(setup_done, 1)

            def steps(order, pair):
                for e in order:
                    op, at = e[0], cnt.step(e)
                    if op == "NO_MASK":
                        V.memset(any_valid[:, :], 1.0)
                        V.memset(mask_add[:, :, :], 0.0).then_inc(dve_step, 1)
                        dve.wait_ge(dve_step, cnt.value("step", at["step"] + 1))
                    elif op == "MASK":
                        dve.wait_ge(mask_landed, dve.snap(pair * 32) + 32)
                        V.tensor_scalar(mask_add[:, :, :], mask_u8[:, :, :], -MASKED, MASKED, ALU.mult, ALU.add)\
                            .then_inc(dve_step, 1)
                        V.tensor_reduce(any_valid[:, :], mask_u8[:, :, :], AX_X, ALU.max).then_inc(dve_step, 1)
                        dve.wait_ge(dve_step, cnt.value("step", at["step"] + 2))
                    elif op == "LN_STATS":
                        b = e[1]
                        if ("x", b) not in made:
                            dve.wait_ge(x_landed[b], dve.snap(pair * 16) + 16)
                        else:
                            ring, n = made["x", b]
                            dve.wait_ge(taken[ring], cnt.value(ring, n + 1 + SLOTS[ring]))
                        for i in range(NT):
                            V.bn_stats(bn[:, b, i, :], x[:, b, i, :]).then_inc(dve_step, 1)
                        for i in range(NT):
                            dve.wait_ge(dve_step, cnt.value("step", at["step"] + i + 1))
                            stand(dve)
                            last = V.bn_aggr(mv[:, b, i, :], bn[:, b, i, :])
                        last.then_inc(stats_done, 1)
                        made["rstd", b] = at["rstd"] + 2
                    elif op == "LN":
                        b = e[1]
                        dve.wait_ge(rstd_done, cnt.value("rstd", made["rstd", b]))
                        for i in range(NT):
                            V.tensor_scalar(xn[:, b, i, :], x[:, b, i, :], mv[:, b, i, 0:1], rstd[:, b, i:i + 1],
                                            ALU.subtract, ALU.mult).then_inc(xn_done, 1)
                    elif op == "ADD_BIAS":
                        b = e[1]
                        dve.wait_ge(xn_done, cnt.value("xn", cnt.n["xn"]))
                        for i in range(NT):
                            last = V.tensor_tensor(x[:, b, i, :], x[:, b, i, :], bias0[:, :], ALU.add)
                        last.then_inc(dve_step, 1)
                        made["biased", b] = at["step"] + 1
                    elif op in ("CT", "XT", "AT", "T", "TV"):
                        dst, src = tile_halves(e, at["t"])
                        low(dst, src, at["hi"], taken["t"])
                    elif op in ("K0", "Q0"):
                        dst, bias = (part(k_t, e[1]), bk) if op == "K0" else (part(q_t, e[1], 0), nbq)
                        dve.wait_ge(hi_done, cnt.value("hi", at["hi"] + 1))
                        V.scalar_tensor_tensor(dst[1], proj_ps[at["pj"] % 2][:, :], bias, dst[0].bitcast(F32),
                                               ALU.add, ALU.subtract).then_inc(taken["pj"], 1)
                    elif op == "K":
                        low(part(k_t, e[1]), proj_ps[at["pj"] % 2][:, :], at["hi"], taken["pj"])
                    elif op == "Q":
                        dst = part(q_t, e[1], e[2])
                        dve.wait_ge(hi_done, cnt.value("hi", at["hi"] + 1))
                        V.scalar_tensor_tensor(dst[1], proj_ps[at["pj"] % 2][:, :], -SCORE_SCALE, dst[0].bitcast(F32),
                                               ALU.mult, ALU.subtract).then_inc(taken["pj"], 1)
                    elif op == "VT":
                        dve.wait_ge(full["pj"], cnt.value("pj", at["pj"] + 1))
                        V.tensor_copy(v_tmp[:, :], proj_ps[at["pj"] % 2][:, :]).then_inc(taken["pj"], 1)
                    elif op in ("E", "S"):
                        b, u, i = (e[1], e[1], e[2]) if op == "E" else e[1:]
                        made["exp", u, i] = at["exp"] + 1
                        dve.wait_ge(full["s"], cnt.value("s", at["s"] + 1))
                        stand(dve)
                        V.tensor_tensor_reduce(out=prob[:, u, i, :], in0=score_ps[at["s"] % 2][:, :],
                                               in1=mask_add[:, b, :], scale=1.0, scalar=MIN_START, op0=ALU.add,
                                               op1=ALU.min, accum_out=smin[:, u, i:i + 1]).then_inc(taken["s"], 1)
                    elif op == "RS":
                        u, b, i = e[1:]
                        dve.wait_ge(exp_done, cnt.value("exp", made["exp", u, i]))
                        V.reciprocal(srec[:, u, i:i + 1], ssum[:, u, i:i + 1]).then_inc(rs_done, 1)
                    elif op == "PV" and e[3] == NT - 1:
                        low(part(o_t, e[1], e[2]), o_ps[:, :], at["hi"], taken["o"])
                    elif op in ("XM", "FC", "Y", "DN"):
                        b, i = e[1:]
                        ring = {"XM": "z", "FC": "z", "Y": "y", "DN": "yf"}[op]
                        n = at[ring]
                        if op == "FC" and i == 0:
                            dve.wait_ge(dve_step, cnt.value("step", made["biased", b]))
                        dve.wait_ge(full[ring], cnt.value(ring, n + 1))
                        V.tensor_tensor(x[:, b, i, :], bank[RINGS[ring][n % SLOTS[ring]]][:, :], x[:, b, i, :], ALU.add)\
                            .then_inc(taken[ring], 1)
                        made["x", b] = ring, n
                    elif op == "GU":
                        b, r = e[1:]
                        dve.wait_ge(h_split, cnt.value("hs", cnt.n.get("kept", 0) + 1 + r))
                        dve.wait_ge(silu_done, cnt.value("sg", at["sg"] + 1))
                        V.tensor_tensor(h_f[:, r, :], up_ps[at["gu"] % 2][:, :], silu[:, at["gu"] % 2, :], ALU.mult)\
                            .then_inc(taken["gu"], 1)
                        made["ab", r] = at["ab"] + 1
                    elif op == "CMP":
                        compare(e[2], at["step"])
                    elif op == "KEEP":
                        keep_two_of_four(at["step"])

            c01, c02, c12, c03, c13, c23, t0, t1, t2, t3, t4, t5 = (flags[:, k, :] for k in range(12))

            def after(k):
                dve.wait_ge(dve_step, cnt.value("step", k))

            def mark(ins):
                ins.then_inc(dve_step, 1)

            def compare(r, k):
                dve.wait_ge(abs_done, cnt.value("ab", made["ab", r]))
                first = r * (r - 1) // 2
                mark(V.tensor_tensor(flags[:, first:first + r, :], h_abs[:, 0:r, :],
                                     h_abs[:, r:r + 1, :].to_broadcast([P, r, S]), ALU.is_ge))
                if r == 2:
                    after(k + 1)
                    mark(V.tensor_tensor(t0, c01, c02, ALU.add))
                    mark(V.tensor_tensor(t2, c02, c12, ALU.add))

            def keep_two_of_four(k):
                compare(3, k)
                after(k + 1)
                mark(V.tensor_tensor(t4, t0, c03, ALU.add))
                mark(V.tensor_tensor(t1, c12, c13, ALU.add))
                mark(V.tensor_tensor(t3, c03, c13, ALU.add))
                after(k + 2)
                keep(0, t4, 1.5, ALU.is_gt)
                after(k + 3)
                mark(V.tensor_tensor(t5, t1, c01, ALU.subtract))
                after(k + 4)
                mark(V.tensor_tensor(c03, t3, c23, ALU.add))
                after(k + 5)
                keep(1, t5, 0.5, ALU.is_gt)
                mark(V.tensor_tensor(c12, t2, c23, ALU.subtract))
                after(k + 6)
                keep(3, c03, 1.5, ALU.is_lt)
                after(k + 7)
                keep(2, c12, 0.5, ALU.is_lt)

            def keep(r, t, bound, test):
                V.scalar_tensor_tensor(h_f[:, r, :], t, bound, h_f[:, r, :], test, ALU.mult).then_inc(kept_done, 1)

            run(dve, cnt, steps)
    return nc


_INS = ["x", "ctx_1024", "mask_BxS2_bf1", "L0_xattn_Wq", "L0_xattn_bq", "L0_xattn_Wk", "L0_xattn_bk", "L0_ffn_weight",
        "L0_ffn_bias", "L1_xattn_Wq", "L1_xattn_Wk", "L1_xattn_Wv", "L1_xattn_Wo", "L1_ffn_w_gate", "L1_ffn_w_up",
        "L1_ffn_w_down"]


def kernel(**inputs):
    import numpy as np
    import concourse.bacc as bacc
    from concourse.bass_utils import run_bass_kernel_spmd

    nc = bacc.Bacc("TRN2", target_bir_lowering=False, num_devices=1)
    arrays, args = {}, []
    for name in _INS:
        a = np.ascontiguousarray(inputs[name])
        if a.dtype == np.bool_:
            a = a.view(np.uint8)
        arrays[f"in_{name}"] = a
        args.append(nc.dram_tensor(f"in_{name}", a.shape, mybir.dt.from_np(a.dtype), kind="ExternalInput").ap())
    out = nc.dram_tensor("out", (B, S, D), F32, kind="ExternalOutput").ap()
    build(nc, *args, out)
    r = run_bass_kernel_spmd(nc, [arrays], core_ids=[0])
    return r.results[0]["out"]
```
